# Optimizing a Trainium2 kernel written in Bass

```python
import numpy as np
import jax
import jax.numpy as jnp

def _softmax(x, axis=-1):
    return jax.nn.softmax(x, axis=axis)

def _gelu(x):
    return jax.nn.gelu(x, approximate=True)

def _silu(x):
    return jax.nn.silu(x)

def _sigmoid(x):
    return jax.nn.sigmoid(x)

def _layernorm(x, axis=-1, eps=1e-05):
    m = jnp.mean(x, axis=axis, keepdims=True)
    v = jnp.var(x, axis=axis, keepdims=True)
    return (x - m) / jnp.sqrt(v + eps)

def _scatter_add(tgt, idx, src, axis=0):
    return tgt.at[idx].add(src)

def _segment_sum(src, seg, n):
    return jax.ops.segment_sum(src, seg, n)
kernel_name = 'mk_decoder_preln_d1_seqx_r8_37119e'

def setup_inputs(seed: int=0):
    np.random.seed(seed)
    _w = jnp.asarray

    def _rec_inputs():
        import jax
        import jax.numpy as jnp
        _rk = jax.random.key(seed)
        x = -0.0002928 + 1 * jax.random.normal(jax.random.fold_in(_rk, 1), (128, 64, 128), jnp.float32)
        _lenS = 64 - jax.random.randint(jax.random.fold_in(_rk, 7), (128,), 0, max(1, 64 // 4) + 1, jnp.int32)
        _lenS2 = 64 - jax.random.randint(jax.random.fold_in(_rk, 8), (128,), 0, max(1, 64 // 4) + 1, jnp.int32)
        _ctx_1024P = jax.random.normal(jax.random.fold_in(_rk, 11), (128, 16, 128), jnp.float32)
        _ctx_1024c = jax.random.dirichlet(jax.random.fold_in(_rk, 511), 0.3 * jnp.ones((16,), jnp.float32), (128, 64))
        _ctx_1024t = jnp.einsum('bsk,bkd->bsd', _ctx_1024c, _ctx_1024P)
        _ctx_1024t = _ctx_1024t * jax.lax.rsqrt(jnp.mean(jnp.square(_ctx_1024t)) + 1e-12) * 0.953939
        ctx_1024 = -1.39393e-06 + 0.999914 * (_ctx_1024t + 0.3 * jax.random.normal(jax.random.fold_in(_rk, 611), (128, 64, 128), jnp.float32))
        return (x, ctx_1024)
    x, ctx_1024 = _rec_inputs()

    def _L0_attn_setup():
        import math
        import jax, jax.numpy as jnp
        import numpy as np
        D_MODEL = 128
        N_HEADS = 16
        D_HEAD = D_MODEL // N_HEADS
        BLOCK = 256
        BATCH = 2
        SEQ = 256

        def _rotate(t, cos, sin):
            t1 = t[..., 0::2]
            t2 = t[..., 1::2]
            r1 = t1 * cos - t2 * sin
            r2 = t1 * sin + t2 * cos
            return jnp.stack([r1, r2], axis=-1).reshape(t.shape)
        key = jax.random.key(seed)
        k1, k2, k3 = jax.random.split(key, 3)
        x = jax.random.normal(k1, (BATCH, SEQ, D_MODEL), dtype=jnp.float32)
        Wqkv = jax.random.normal(k2, (3 * D_MODEL, D_MODEL), dtype=jnp.float32) * 0.02
        Wo = jax.random.normal(k3, (D_MODEL, D_MODEL), dtype=jnp.float32) * 0.02
        log_xi = jnp.full((N_HEADS,), math.log(BLOCK / 2.0), dtype=jnp.float32)
        pi_gate_logit = jnp.full((N_HEADS,), 2.0, dtype=jnp.float32)
        e_gate_logit = jnp.full((N_HEADS,), 2.0, dtype=jnp.float32)
        return {'x': x, 'Wqkv': Wqkv, 'Wo': Wo, 'log_xi': log_xi, 'pi_gate_logit': pi_gate_logit, 'e_gate_logit': e_gate_logit}
    _L0_attn_all = _L0_attn_setup()
    _L0_attn_in = {k: v for k, v in _L0_attn_all.items() if k in ('Wqkv', 'Wo', 'log_xi', 'pi_gate_logit', 'e_gate_logit')}
    del _L0_attn_all

    def _L0_xattn_setup():
        import jax, jax.numpy as jnp
        import numpy as np
        D_MODEL = 128
        N_HEADS = 16
        D_K = D_MODEL // N_HEADS

        def _split_heads(x, bs):
            return x.reshape(bs, -1, N_HEADS, D_K).transpose(0, 2, 1, 3)
        key = jax.random.key(seed)
        ks = jax.random.split(key, 11)
        bs, seq = (2, 256)
        s = 1.0 / np.sqrt(D_MODEL)
        return {'q': jax.random.normal(ks[0], (bs, seq, D_MODEL), jnp.float32), 'k': jax.random.normal(ks[1], (bs, seq, D_MODEL), jnp.float32), 'v': jax.random.normal(ks[2], (bs, seq, D_MODEL), jnp.float32), 'W_q': jax.random.normal(ks[3], (D_MODEL, D_MODEL), jnp.float32) * s, 'b_q': jnp.zeros((D_MODEL,), jnp.float32), 'W_k': jax.random.normal(ks[4], (D_MODEL, D_MODEL), jnp.float32) * s, 'b_k': jnp.zeros((D_MODEL,), jnp.float32), 'W_v': jax.random.normal(ks[5], (D_MODEL, D_MODEL), jnp.float32) * s, 'b_v': jnp.zeros((D_MODEL,), jnp.float32), 'W_o': jax.random.normal(ks[6], (D_MODEL, D_MODEL), jnp.float32) * s, 'b_o': jnp.zeros((D_MODEL,), jnp.float32)}
    _L0_xattn_all = _L0_xattn_setup()
    _L0_xattn_in = {k: v for k, v in _L0_xattn_all.items() if k in ('W_q', 'b_q', 'W_k', 'b_k', 'W_v', 'b_v', 'W_o', 'b_o')}
    del _L0_xattn_all

    def _L0_ffn_setup():
        import jax, jax.numpy as jnp
        import numpy as np
        DIM = 128
        HIDDEN = 384
        SCALE = 1.0 / 127.0

        def _dequant(w_int, dtype):
            return w_int.astype(dtype) * jnp.asarray(SCALE, dtype)
        key = jax.random.key(seed)
        k_x, k_g, k_u, k_d = jax.random.split(key, 4)
        x = jax.random.normal(k_x, (4, 256, DIM), dtype=jnp.float32)
        w_gate = jax.random.randint(k_g, (HIDDEN, DIM), -127, 128, dtype=jnp.int32)
        w_up = jax.random.randint(k_u, (HIDDEN, DIM), -127, 128, dtype=jnp.int32)
        w_down = jax.random.randint(k_d, (DIM, HIDDEN), -127, 128, dtype=jnp.int32)
        return {'x': x, 'w_gate': w_gate, 'w_up': w_up, 'w_down': w_down}
    _L0_ffn_all = _L0_ffn_setup()
    _L0_ffn_in = {k: v for k, v in _L0_ffn_all.items() if k in ('w_gate', 'w_up', 'w_down')}
    del _L0_ffn_all
    return {'x': x, 'ctx_1024': ctx_1024, 'L0_attn_Wqkv': _L0_attn_in['Wqkv'], 'L0_attn_Wo': _L0_attn_in['Wo'], 'L0_attn_log_xi': _L0_attn_in['log_xi'], 'L0_attn_pi_gate_logit': _L0_attn_in['pi_gate_logit'], 'L0_attn_e_gate_logit': _L0_attn_in['e_gate_logit'], 'L0_xattn_W_q': _L0_xattn_in['W_q'], 'L0_xattn_b_q': _L0_xattn_in['b_q'], 'L0_xattn_W_k': _L0_xattn_in['W_k'], 'L0_xattn_b_k': _L0_xattn_in['b_k'], 'L0_xattn_W_v': _L0_xattn_in['W_v'], 'L0_xattn_b_v': _L0_xattn_in['b_v'], 'L0_xattn_W_o': _L0_xattn_in['W_o'], 'L0_xattn_b_o': _L0_xattn_in['b_o'], 'L0_ffn_w_gate': _L0_ffn_in['w_gate'], 'L0_ffn_w_up': _L0_ffn_in['w_up'], 'L0_ffn_w_down': _L0_ffn_in['w_down']}

def reference(x, ctx_1024, L0_attn_Wqkv, L0_attn_Wo, L0_attn_log_xi, L0_attn_pi_gate_logit, L0_attn_e_gate_logit, L0_xattn_W_q, L0_xattn_b_q, L0_xattn_W_k, L0_xattn_b_k, L0_xattn_W_v, L0_xattn_b_v, L0_xattn_W_o, L0_xattn_b_o, L0_ffn_w_gate, L0_ffn_w_up, L0_ffn_w_down):
    import jax
    import jax.numpy as jnp

    def _L0_attn_ref(x, Wqkv, Wo, log_xi, pi_gate_logit, e_gate_logit):
        import math
        import jax, jax.numpy as jnp
        import numpy as np
        D_MODEL = 128
        N_HEADS = 16
        D_HEAD = D_MODEL // N_HEADS
        BLOCK = 256
        BATCH = 2
        SEQ = 256

        def _rotate(t, cos, sin):
            t1 = t[..., 0::2]
            t2 = t[..., 1::2]
            r1 = t1 * cos - t2 * sin
            r2 = t1 * sin + t2 * cos
            return jnp.stack([r1, r2], axis=-1).reshape(t.shape)
        b, n, d = x.shape
        H, dh = (N_HEADS, D_HEAD)
        qkv = (x @ Wqkv.T).reshape(b, n, 3, H, dh)
        q = jnp.transpose(qkv[:, :, 0], (0, 2, 1, 3))
        k = jnp.transpose(qkv[:, :, 1], (0, 2, 1, 3))
        v = jnp.transpose(qkv[:, :, 2], (0, 2, 1, 3))
        pi_g = jax.nn.sigmoid(pi_gate_logit)
        e_g = jax.nn.sigmoid(e_gate_logit)
        kfrac = jnp.arange(0, dh, 2, dtype=jnp.float32) / dh
        pi_inv_freq = jnp.float32(math.pi) ** (1.0 - kfrac)
        pos = jnp.arange(n, dtype=jnp.float32)
        theta = pos[:, None] * pi_inv_freq[None, :]
        theta = theta[None, :, :] * pi_g[:, None, None]
        cos, sin = (jnp.cos(theta), jnp.sin(theta))
        q_rot = _rotate(q, cos, sin)
        k_rot = _rotate(k, cos, sin)
        scores = jnp.einsum('bhqd,bhkd->bhqk', q_rot, k_rot) / jnp.float32(math.sqrt(dh))
        xi = jnp.exp(log_xi)
        i = jnp.arange(n, dtype=jnp.float32)
        d_mat = jnp.abs(i[:, None] - i[None, :])
        decay_bias = -(d_mat[None, :, :] / xi[:, None, None]) * e_g[:, None, None]
        scores = scores + decay_bias[None]
        causal = jnp.tril(jnp.ones((n, n), dtype=bool))
        scores = jnp.where(causal[None, None], scores, jnp.float32(-jnp.inf))
        attn = jax.nn.softmax(scores, axis=-1)
        out = jnp.einsum('bhqk,bhkd->bhqd', attn, v)
        out = jnp.transpose(out, (0, 2, 1, 3)).reshape(b, n, d)
        return out @ Wo.T

    def _L0_xattn_ref(q, k, v, W_q, b_q, W_k, b_k, W_v, b_v, W_o, b_o):
        import jax, jax.numpy as jnp
        import numpy as np
        D_MODEL = 128
        N_HEADS = 16
        D_K = D_MODEL // N_HEADS

        def _split_heads(x, bs):
            return x.reshape(bs, -1, N_HEADS, D_K).transpose(0, 2, 1, 3)
        bs = q.shape[0]
        qh = _split_heads(q @ W_q.T + b_q, bs)
        kh = _split_heads(k @ W_k.T + b_k, bs)
        vh = _split_heads(v @ W_v.T + b_v, bs)
        scores = jnp.einsum('bhqd,bhkd->bhqk', qh, kh) / jnp.sqrt(jnp.float32(D_K))
        weight = jax.nn.softmax(scores, axis=-1)
        attn = jnp.einsum('bhqk,bhkd->bhqd', weight, vh)
        concat = attn.transpose(0, 2, 1, 3).reshape(bs, -1, D_MODEL)
        return concat @ W_o.T + b_o

    def _L0_ffn_ref(x, w_gate, w_up, w_down):
        import jax, jax.numpy as jnp
        import numpy as np
        DIM = 128
        HIDDEN = 384
        SCALE = 1.0 / 127.0

        def _dequant(w_int, dtype):
            return w_int.astype(dtype) * jnp.asarray(SCALE, dtype)
        wg = _dequant(w_gate, x.dtype)
        wu = _dequant(w_up, x.dtype)
        wd = _dequant(w_down, x.dtype)
        gate = jnp.einsum('bsd,hd->bsh', x, wg)
        up = jnp.einsum('bsd,hd->bsh', x, wu)
        h = jax.nn.silu(gate) * up
        return jnp.einsum('bsh,dh->bsd', h, wd)
    x = x + _L0_attn_ref(_layernorm(x, axis=-1), L0_attn_Wqkv, L0_attn_Wo, L0_attn_log_xi, L0_attn_pi_gate_logit, L0_attn_e_gate_logit)
    x = x + _L0_xattn_ref(_layernorm(x, axis=-1), ctx_1024, ctx_1024, L0_xattn_W_q, L0_xattn_b_q, L0_xattn_W_k, L0_xattn_b_k, L0_xattn_W_v, L0_xattn_b_v, L0_xattn_W_o, L0_xattn_b_o)
    x = x + _L0_ffn_ref(_layernorm(x, axis=-1), L0_ffn_w_gate, L0_ffn_w_up, L0_ffn_w_down)
    return x

_drawn_inputs = setup_inputs


def setup_inputs(seed=0):
    import zlib

    import numpy as np

    out = dict(_drawn_inputs(seed))
    spreads = {'L0_attn_log_xi': (4.852030277252197, 0.6),
     'L0_attn_pi_gate_logit': (2.0, 0.6),
     'L0_attn_e_gate_logit': (2.0, 0.6),
     'L0_xattn_b_q': (0.0, 0.1),
     'L0_xattn_b_k': (0.0, 0.8),
     'L0_xattn_b_v': (0.0, 0.1),
     'L0_xattn_b_o': (0.0, 0.1)}
    factors = {'L0_attn_Wqkv': 3.165, 'L0_attn_Wo': 3.14}
    for name, (base, spread) in spreads.items():
        noise = np.random.default_rng([zlib.crc32(name.encode()), seed]).standard_normal(out[name].shape)
        drawn = base * np.exp(spread * noise) if base else spread * noise
        out[name] = jnp.asarray(drawn.astype(out[name].dtype))
    for name, factor in factors.items():
        out[name] = (out[name] * factor).astype(out[name].dtype)
    return out
```

```python
from contextlib import ExitStack

import numpy as np
import concourse.bass as bass
from concourse import mybir

F32 = mybir.dt.float32
F16 = mybir.dt.float16
BF16 = mybir.dt.bfloat16
I32 = mybir.dt.int32
ALU = mybir.AluOpType
ACT = mybir.ActivationFunctionType
AX = mybir.AxisListType

BATCH, SEQ, D = 128, 64, 128
HEADS, DH = 16, 8
HIDDEN = 384
CHUNKS = HIDDEN // 128
TOK = 2 * SEQ
PAIRS = BATCH * SEQ // TOK
SLOT = 32
GROUPS = HEADS * SLOT // 128
HPAIRS = HEADS // 2
EPS = 1e-5
SCORE_SCALE = float(DH) ** -0.5
DEQUANT = 1.0 / 127.0
MASKED = -1e30
MAX_DECAY = 336.0
SHIFT_ROWS = 2 * HEADS + SEQ
STAGES = 5
PEELED = 6
TWO_PI = 2 * np.pi
TWO_PI_HIGH = 6.28125
ROUND = 1.5 * 2.0 ** 23


class Record:
    pass


def constants():
    tok = np.arange(TOK)
    k = tok % SEQ
    bf = mybir.dt.np(BF16)
    future = np.where(np.arange(SEQ)[:, None] > k[None, :], MASKED, 0.0)
    shift_pick = np.zeros((SHIFT_ROWS, HPAIRS, 2, SEQ), np.float32)
    for h in range(HEADS):
        shift_pick[h, h // 2, h % 2] = 1
        shift_pick[HEADS + h, h // 2, h % 2] = 1
    for j in range(SEQ):
        shift_pick[2 * HEADS + j, :, :, j] = 1
    ones = np.zeros((2, SEQ, 2, 4, DH), np.float32)
    for h2 in range(2):
        for i in range(2):
            ones[h2, :, i, 2 * i + h2] = 1
    freq = np.float32(np.pi) ** (np.float32(1) - np.arange(0, DH, 2, dtype=np.float32) / np.float32(DH))
    return {
        "c_ident": np.eye(128, dtype=np.float32),
        "c_ident16": np.eye(128, dtype=np.float16),
        "c_identb": np.eye(128).astype(bf),
        "c_future": future.astype(bf),
        "c_key_is": np.tile(np.eye(SEQ), (1, 8)).astype(bf),
        "c_shift_pick": shift_pick.reshape(SHIFT_ROWS, HPAIRS * 128).astype(bf),
        "c_ones": ones.reshape(128, 2 * 4 * DH),
        "c_angle": (k[:, None].astype(np.float32) * freq[None, :].astype(np.float32)),
        "c_kpos": k[:, None].astype(np.float32),
        "c_part": np.eye(3, dtype=np.float32),
    }


def build(nc, a, out):
    x_d = a["x"].rearrange("(p t) d -> t p d", t=TOK)
    out_d = out.rearrange("(p t) d -> t p d", t=TOK)

    with ExitStack() as ctx:
        def sb(name, shape, dt=F32):
            return ctx.enter_context(nc.sbuf_tensor(name, shape, dt))

        def sem(name):
            return ctx.enter_context(nc.semaphore(name))

        psum = ctx.enter_context(nc.psum_tensor("psum", [128, 8, 512], F32))

        ident = sb("ident", [128, 128])
        ident16 = sb("ident16", [128, 128], F16)
        identb = sb("identb", [128, 128], BF16)
        future = sb("future", [SEQ, TOK], BF16)
        key_is = sb("key_is", [SEQ, 512], BF16)
        shift_pick = sb("shift_pick", [SHIFT_ROWS, HPAIRS, 128], BF16)
        ones = sb("ones", [128, 2, 4 * DH])
        angle = sb("angle", [128, DH // 2])
        kpos = sb("kpos", [128, 1])
        part = sb("part", [3, 3])
        w_self = sb("w_self", [128, 3 * D])
        w_self_out = sb("w_self_out", [128, D])
        w_cross = sb("w_cross", [128, 3 * D])
        w_cross_out = sb("w_cross_out", [128, D])
        w_int = sb("w_int", [128, 3, HIDDEN], I32)
        w_ffn = sb("w_ffn", [128, 3, HIDDEN])
        gates = sb("gates", [128, 3, HEADS])
        biases = sb("biases", [3, 5 * D])
        bias_rest = sb("bias_rest", [3, 5 * D])
        bias_cut = sb("bias_cut", [3, 3, 5 * D], BF16)
        bias_sum = sb("bias_sum", [3, 2, 5 * D])
        bias_parts = sb("bias_parts", [3, 5 * D], BF16)
        one_rows = sb("one_rows", [3, TOK], BF16)
        minus_half = sb("minus_half", [128, 1])
        eps = sb("eps", [128, 1])

        gate_tanh = sb("gate_tanh", [128, 3, HEADS])
        gate = sb("gate", [128, 3, HEADS])
        inv_xi = sb("inv_xi", [128, HEADS])
        theta = sb("theta", [128, HEADS, DH // 2])
        turns = sb("turns", [128, 2, HEADS, DH // 2])
        reduced = sb("reduced", [128, 2, HEADS, DH // 2])
        sincos = sb("sincos", [128, 2, HEADS, DH // 2])
        rot_cos = sb("rot_cos", [128, HEADS * DH // 2, 2])
        rot_sin = sb("rot_sin", [128, HEADS * DH // 2, 2])
        decay = sb("decay", [128, HEADS])
        decay_rest = sb("decay_rest", [128, 2, HEADS])

        x_all = sb("x_all", [128, PAIRS * D])
        context = sb("context", [128, 2, D])

        const_loaded = sem("const_loaded")
        x_first_loaded = sem("x_first_loaded")
        x_rest_loaded = sem("x_rest_loaded")
        slots_cleared = sem("slots_cleared")
        dve_setup = sem("dve_setup")
        act_setup = sem("act_setup")
        angles_ready = sem("angles_ready")
        setup_done = sem("setup_done")
        context_loaded = [sem(f"context_loaded{u}") for u in range(2)]
        stored = sem("stored")

        def norm_state(n):
            s = Record()
            s.stats = sb(f"{n}_stats", [128, 6])
            s.moments = sb(f"{n}_moments", [128, 2])
            s.var_eps = sb(f"{n}_var_eps", [128, 1])
            s.rstd = sb(f"{n}_rstd", [128, 1])
            s.normed = sb(f"{n}_normed", [128, D])
            s.moments_ready = sem(f"{n}_moments_ready")
            s.var_ready = sem(f"{n}_var_ready")
            s.rstd_ready = sem(f"{n}_rstd_ready")
            s.normed_ready = sem(f"{n}_normed_ready")
            return s

        def attention_state(n, bank, score_bank):
            s = Record()
            s.causal, s.norm = n == "self", norm_state(n)
            s.lin, s.scores = psum[:, bank, :], psum[:, score_bank:score_bank + 2, :]
            s.inputsT = sb(f"{n}_inputsT", [128, 2, TOK])
            s.slots = sb(f"{n}_slots", [128, 2, HEADS, SLOT], F16)
            s.stacked = sb(f"{n}_stacked", [128, 2, 2, GROUPS * TOK], F16)
            s.key_diag = sb(f"{n}_key_diag", [128, 2, 2 * GROUPS, 4, SEQ], F16)
            s.values = sb(f"{n}_values", [128, 2, 8, 4, 2 * DH])
            s.neg_max = sb(f"{n}_neg_max", [128, HEADS])
            s.max_parts = sb(f"{n}_max_parts", [128, 2, HEADS], BF16)
            s.shift = sb(f"{n}_shift", [SHIFT_ROWS, TOK], BF16)
            s.probs = sb(f"{n}_probs", [128, HPAIRS * TOK])
            s.inv_sum = sb(f"{n}_inv_sum", [128, TOK])
            s.mixedT = sb(f"{n}_mixedT", [128, TOK])
            s.inputs_turned = sem(f"{n}_inputs_turned")
            s.inputsT_ready = sem(f"{n}_inputsT_ready")
            s.qkv_ready = sem(f"{n}_qkv_ready")
            s.rotated_a = sem(f"{n}_rotated_a")
            s.rotated = sem(f"{n}_rotated")
            s.high_ready = sem(f"{n}_high_ready")
            s.values_ready = sem(f"{n}_values_ready")
            s.low_ready = sem(f"{n}_low_ready")
            s.slots_turned = sem(f"{n}_slots_turned")
            s.stacked_ready = sem(f"{n}_stacked_ready")
            s.scores_ready = sem(f"{n}_scores_ready")
            s.max_ready = sem(f"{n}_max_ready")
            s.max_high_ready = sem(f"{n}_max_high_ready")
            s.max_split = sem(f"{n}_max_split")
            s.max_turned = sem(f"{n}_max_turned")
            s.shift_ready = sem(f"{n}_shift_ready")
            s.scoresT_ready = sem(f"{n}_scoresT_ready")
            s.probs_ready = sem(f"{n}_probs_ready")
            s.mixed_ready = sem(f"{n}_mixed_ready")
            s.inv_sum_ready = sem(f"{n}_inv_sum_ready")
            s.mixedT_ready = sem(f"{n}_mixedT_ready")
            s.projected = sem(f"{n}_projected")
            s.x_updated = sem(f"{n}_x_updated")
            s.diag_ready = [sem(f"{n}_diag_ready{u}") for u in range(2)]
            return s

        A = attention_state("self", 4, 0)
        B = attention_state("cross", 5, 2)
        rot_a = sb("rot_a", [128, 2 * D // 2, 2])
        rot_b = sb("rot_b", [128, 2 * D // 2, 2])
        rot = sb("rot", [128, 2, HEADS, DH])
        F = Record()
        F.norm = norm_state("ffn")
        F.gate, F.up = psum[:, 6, :], psum[:, 7, :]
        F.inputT = sb("ffn_inputT", [128, TOK])
        F.tanh = sb("ffn_tanh", [128, HIDDEN])
        F.gated = sb("ffn_gated", [128, HIDDEN])
        F.hidden = sb("ffn_hidden", [128, HIDDEN])
        F.input_turned = sem("ffn_input_turned")
        F.inputT_ready = sem("ffn_inputT_ready")
        F.gate_up_ready = sem("ffn_gate_up_ready")
        F.tanh_ready = sem("ffn_tanh_ready")
        F.gated_ready = sem("ffn_gated_ready")
        F.hidden_ready = sem("ffn_hidden_ready")
        F.down_ready = sem("ffn_down_ready")
        F.x_updated = sem("ffn_x_updated")

        def pair_of(t, stage, i):
            p = Record()
            p.n0 = t - stage
            p.u = p.n0 % 2
            p.live = i is not None or 0 <= p.n0 < PAIRS
            p.n = p.n0 if i is None else p.n0 + 2 * i
            p.half = p.n0 // 2 if i is None else p.n0 // 2 + i
            return p

        def run(eng, step):
            for t in range(PEELED):
                step(lambda s, t=t: pair_of(t, s, None))
            with eng.Fori(0, (PAIRS - PEELED) // 2) as i:
                for u in range(2):
                    step(lambda s, u=u: pair_of(PEELED + u, s, i))
            for t in range(PAIRS, PAIRS + STAGES - 1):
                step(lambda s, t=t: pair_of(t, s, None))

        def before(eng, semaphore, p, back=1):
            if p.n0 >= back:
                eng.wait_ge(semaphore, p.n + 1 - back)

        def now(eng, semaphore, p):
            eng.wait_ge(semaphore, p.n + 1)

        def x_of(p):
            return x_all[:, bass.ds(p.n * D, D)]

        block = ctx.enter_context(nc.Block())

        N_CONST = 27
        @block.sync
        def _(sp):
            for dst, src in (
                    (gates[:, 0, :], a["log_xi"].partition_broadcast(128)),
                    (gates[:, 1, :], a["pi_gate"].partition_broadcast(128)),
                    (gates[:, 2, :], a["e_gate"].partition_broadcast(128)),
                    (angle[:], a["c_angle"]), (kpos[:], a["c_kpos"]), (part[:], a["c_part"]),
                    (ident[:], a["c_ident"]), (ident16[:], a["c_ident16"]), (identb[:], a["c_identb"]),
                    (future[:], a["c_future"]), (key_is[:], a["c_key_is"]),
                    (shift_pick[:].rearrange("p a b -> p (a b)"), a["c_shift_pick"]),
                    (ones[:].rearrange("p a b -> p (a b)"), a["c_ones"]),
                    (w_self[:], a["w_qkvT"]), (w_self_out[:], a["w_self_outT"]),
                    (w_cross[:, 0:D], a["w_qT"]), (w_cross[:, D:2 * D], a["w_kT"]),
                    (w_cross[:, 2 * D:3 * D], a["w_vT"]), (w_cross_out[:], a["w_cross_outT"]),
                    (w_int[:, 0, :], a["w_gateT"]), (w_int[:, 1, :], a["w_upT"]),
                    (w_int[:, 2, :].rearrange("p (c d) -> p c d", c=CHUNKS),
                     a["w_downT"].rearrange("(c p) d -> p c d", c=CHUNKS)),
                    (biases[:, 0:D], a["b_q"].partition_broadcast(3)),
                    (biases[:, D:2 * D], a["b_k"].partition_broadcast(3)),
                    (biases[:, 2 * D:3 * D], a["b_v"].partition_broadcast(3)),
                    (biases[:, 3 * D:4 * D], a["b_v"].partition_broadcast(3)),
                    (biases[:, 4 * D:5 * D], a["b_o"].partition_broadcast(3))):
                sp.dma_start(dst, src).then_inc(const_loaded, 16)

            def load_context(p):
                before(sp, B.inputs_turned, p, 2)
                sp.dma_start(context[:, p.u, :], a["ctx"][bass.ds(p.n * TOK, TOK), :]).then_inc(context_loaded[p.u], 16)

            def spread_keys(s, p):
                now(sp, s.stacked_ready, p)
                before(sp, s.scoresT_ready, p, 2)
                for h in range(4):
                    rows = slice(SLOT * h, SLOT * (h + 1))
                    sp.dma_start(s.key_diag[rows, p.u, :, h, :], s.stacked[rows, p.u, 1, :].rearrange("p (n k) -> p n k", k=SEQ)).then_inc(s.diag_ready[p.u], 16)

            def store(p):
                now(sp, F.x_updated, p)
                sp.dma_start(a["out_flat"][bass.ds(p.n * TOK, TOK), :], x_of(p)).then_inc(stored, 16)

            sp.wait_ge(slots_cleared, 1)

            def step(pair):
                p = pair(1)
                if p.live:
                    load_context(p)
                p = pair(4)
                if p.live:
                    store(p)
                p = pair(0)
                if p.live:
                    spread_keys(A, p)
                p = pair(2)
                if p.live:
                    spread_keys(B, p)

            run(sp, step)
            sp.wait_ge(stored, 16 * PAIRS)

        @block.gpsimd
        def _(pool):
            pool.memset(minus_half[:], -0.5)
            pool.memset(eps[:], EPS)
            pool.memset(A.values[:], 0.0)
            pool.memset(B.values[:], 0.0)
            pool.memset(A.key_diag[:], 0.0)
            pool.memset(B.key_diag[:], 0.0).then_inc(slots_cleared, 1)
            pool.wait_ge(slots_cleared, 1)

            def rstd(n, p):
                now(pool, n.moments_ready, p)
                pool.tensor_tensor(n.var_eps[:], n.moments[:, 1:2], eps[:], ALU.add).then_inc(n.var_ready, 1)
                now(pool, n.var_ready, p)
                pool.tensor_tensor(n.rstd[:], n.var_eps[:], minus_half[:], ALU.pow).then_inc(n.rstd_ready, 1)

            def add_rotation(p):
                now(pool, A.rotated_a, p)
                before(pool, A.high_ready, p)
                before(pool, A.low_ready, p)
                pool.tensor_tensor(rot[:].rearrange("p a h d -> p (a h d)"), rot_a[:].rearrange("p a b -> p (a b)"),
                                   rot_b[:].rearrange("p a b -> p (a b)"), ALU.add).then_inc(A.rotated, 1)

            def split_low(p):
                now(pool, A.high_ready, p)
                pool.tensor_tensor(A.slots[:, 0, :, 16:24], rot[:, 0], A.slots[:, 0, :, 0:8], ALU.subtract)
                pool.tensor_tensor(A.slots[:, 1, :, 8:16], rot[:, 1], A.slots[:, 1, :, 0:8], ALU.subtract).then_inc(A.low_ready, 1)

            def step(pair):
                p = pair(0)
                if p.live:
                    rstd(A.norm, p)
                p = pair(2)
                if p.live:
                    rstd(B.norm, p)
                p = pair(4)
                if p.live:
                    rstd(F.norm, p)
                p = pair(0)
                if p.live:
                    add_rotation(p)
                    split_low(p)

            run(pool, step)

        @block.scalar
        def _(act):
            act.dma_start(x_all[:, 0:4 * D].rearrange("t (p d) -> t p d", d=D), x_d[:, 0:4, :]).then_inc(x_first_loaded, 16)
            act.dma_start(x_all[:, 4 * D:].rearrange("t (p d) -> t p d", d=D), x_d[:, 4:PAIRS, :]).then_inc(x_rest_loaded, 16)
            act.wait_ge(const_loaded, 16 * N_CONST)
            act.activation(inv_xi[:], gates[:, 0, :], ACT.Exp, scale=-1.0)
            act.activation(gate_tanh[:], gates[:], ACT.Tanh, scale=0.5).then_inc(act_setup, 1)
            act.wait_ge(angles_ready, 1)
            act.activation(sincos[:], reduced[:], ACT.Sin).then_inc(act_setup, 1)
            act.wait_ge(setup_done, 1)

            def turn_self_in(p):
                now(act, A.inputs_turned, p)
                act.activation(A.inputsT[:, 0, :], A.lin[:, 0:TOK], ACT.Copy).then_inc(A.inputsT_ready, 1)

            def turn_cross_in(p):
                now(act, B.inputs_turned, p)
                act.activation(B.inputsT[:].rearrange("p a t -> p (a t)"), B.lin[:, 0:2 * TOK], ACT.Copy).then_inc(B.inputsT_ready, 1)

            def turn_ffn_in(p):
                now(act, F.input_turned, p)
                act.activation(F.inputT[:], F.gate[:, 0:TOK], ACT.Copy).then_inc(F.inputT_ready, 1)

            def split_high(s, q, k):
                act.activation(s.slots[:, 0, :, 0:16].rearrange("p h (r d) -> p h r d", d=DH),
                               q.unsqueeze(2).broadcast_to([128, HEADS, 2, DH]), ACT.Copy)
                act.activation(s.slots[:, 1, :, 0:8], k, ACT.Copy)
                act.activation(s.slots[:, 1, :, 16:24], k, ACT.Copy).then_inc(s.high_ready, 1)

            def take_values(s, p):
                before(act, s.mixed_ready, p, 2)
                v = s.lin[:, 2 * D:4 * D].rearrange("p (a i t d) -> p a i t d", i=2, t=2, d=DH)
                for t in range(2):
                    rows = slice(SEQ * t, SEQ * (t + 1))
                    last = act.activation(s.values[rows, p.u, :, 0:4:3, t * DH:(t + 1) * DH], v[rows, :, :, t, :], ACT.Copy)
                last.then_inc(s.values_ready, 1)

            def heads(ap):
                return ap.rearrange("p (h d) -> p h d", d=DH)

            def self_values(p):
                now(act, A.rotated_a, p)
                take_values(A, p)

            def self_high(p):
                now(act, A.rotated, p)
                split_high(A, rot[:, 0], rot[:, 1])

            def cross_high(p):
                now(act, B.qkv_ready, p)
                split_high(B, heads(B.lin[:, 0:D]), heads(B.lin[:, D:2 * D]))
                take_values(B, p)

            def take_shift(s, p):
                now(act, s.max_turned, p)
                before(act, s.scoresT_ready, p)
                turned = s.scores[0:2 * HEADS, 1, 0:TOK // 2].bitcast(BF16)
                act.activation(s.shift[0:2 * HEADS, :], turned, ACT.Copy).then_inc(s.shift_ready, 1)

            def exponent(s, p):
                now(act, s.scoresT_ready, p)
                act.activation(s.probs[:].rearrange("p (b n) -> p b n", b=2), s.scores, ACT.Exp, scale=SCORE_SCALE).then_inc(s.probs_ready, 1)

            def ffn_tanh(p):
                now(act, F.gate_up_ready, p)
                before(act, F.gated_ready, p)
                act.activation(F.tanh[:], F.gate[:, 0:HIDDEN], ACT.Tanh, scale=0.5 * DEQUANT).then_inc(F.tanh_ready, 1)

            def step(pair):
                a0, a1, b0, b1, f = (pair(s) for s in range(5))
                if a0.live:
                    turn_self_in(a0)
                if b0.live:
                    turn_cross_in(b0)
                if f.live:
                    turn_ffn_in(f)
                if a1.live:
                    take_shift(A, a1)
                if a0.live:
                    self_values(a0)
                    self_high(a0)
                if b0.live:
                    cross_high(b0)
                if a1.live:
                    exponent(A, a1)
                if f.live:
                    ffn_tanh(f)
                if b1.live:
                    take_shift(B, b1)
                    exponent(B, b1)

            run(act, step)

        @block.vector
        def _(dve):
            count = [0]

            def done(ins):
                ins.then_inc(dve_setup, 1)
                count[0] += 1
                dve.wait_ge(dve_setup, count[0])

            dve.wait_ge(act_setup, 1)
            done(dve.tensor_scalar(gate[:], gate_tanh[:], 0.5, 0.5, ALU.mult, ALU.add))
            done(dve.tensor_tensor(theta[:], angle[:].unsqueeze(1).broadcast_to([128, HEADS, DH // 2]),
                                   gate[:, 1, :].unsqueeze(2).broadcast_to([128, HEADS, DH // 2]), ALU.mult))
            dve.tensor_scalar(turns[:, 0], theta[:], 1 / TWO_PI, ROUND, ALU.mult, ALU.add)
            done(dve.tensor_scalar(turns[:, 1], theta[:], 1 / TWO_PI, 0.25, ALU.mult, ALU.add))
            done(dve.tensor_scalar(turns[:, 1], turns[:, 1], ROUND, None, ALU.add))
            done(dve.tensor_scalar(turns[:], turns[:], -ROUND, None, ALU.add))
            for n in range(2):
                last = dve.scalar_tensor_tensor(reduced[:, n], turns[:, n], -TWO_PI_HIGH, theta[:], ALU.mult, ALU.add)
            done(last)
            flat = reduced[:].rearrange("p a h i -> p (a h i)")
            done(dve.scalar_tensor_tensor(flat, turns[:].rearrange("p a h i -> p (a h i)"), -(TWO_PI - TWO_PI_HIGH), flat, ALU.mult, ALU.add))
            done(dve.tensor_scalar(reduced[:, 1], reduced[:, 1], np.pi / 2, None, ALU.add))
            dve.tensor_scalar(reduced[:], reduced[:], 3.1415925, -3.1415925, ALU.min, ALU.max).then_inc(angles_ready, 1)
            done(dve.tensor_tensor(decay[:], inv_xi[:], gate[:, 2, :], ALU.mult))
            done(dve.tensor_scalar(decay[:], decay[:], MAX_DECAY, 1 / SCORE_SCALE, ALU.min, ALU.mult))
            done(dve.tensor_scalar(decay[:], decay[:], kpos[:], None, ALU.mult))
            done(dve.memset(A.slots[:], 0.0))
            dve.memset(A.slots[:, 0, :, 24:27], 1.0)
            k1, k2, k3 = (A.slots[:, 1, :, n] for n in (24, 25, 26))
            done(dve.tensor_copy(k1, decay[:]))
            done(dve.tensor_tensor(decay_rest[:, 0], decay[:], k1, ALU.subtract))
            done(dve.tensor_copy(k2, decay_rest[:, 0]))
            done(dve.tensor_tensor(decay_rest[:, 1], decay_rest[:, 0], k2, ALU.subtract))
            dve.tensor_copy(k3, decay_rest[:, 1])
            dve.memset(B.slots[:], 0.0)
            done(dve.tensor_copy(bias_cut[:, 0], biases[:]))
            done(dve.tensor_tensor(bias_rest[:], biases[:], bias_cut[:, 0], ALU.subtract))
            done(dve.tensor_copy(bias_cut[:, 1], bias_rest[:]))
            done(dve.tensor_tensor(bias_rest[:], bias_rest[:], bias_cut[:, 1], ALU.subtract))
            done(dve.tensor_copy(bias_cut[:, 2], bias_rest[:]))
            done(dve.tensor_scalar(bias_sum[:, 0], bias_cut[:, 0], part[:, 0:1], None, ALU.mult))
            done(dve.scalar_tensor_tensor(bias_sum[:, 1], bias_cut[:, 1], part[:, 1:2], bias_sum[:, 0], ALU.mult, ALU.add))
            dve.scalar_tensor_tensor(bias_parts[:], bias_cut[:, 2], part[:, 2:3], bias_sum[:, 1], ALU.mult, ALU.add)
            dve.memset(one_rows[:], 1.0)
            dve.memset(B.shift[:], 0.0)
            dve.tensor_copy(A.shift[32:64, :], future[0:32, :])
            dve.tensor_copy(A.shift[64:96, :], future[32:64, :])
            dve.tensor_copy(w_ffn[:], w_int[:])
            dve.wait_ge(act_setup, 2)
            sin = sincos[:, 0].rearrange("p h i -> p (h i)")
            cos = sincos[:, 1].rearrange("p h i -> p (h i)")
            dve.tensor_copy(rot_cos[:, :, 0], cos)
            dve.tensor_copy(rot_cos[:, :, 1], cos)
            dve.tensor_scalar(rot_sin[:, :, 0], sin, -1.0, None, ALU.mult)
            done(dve.tensor_copy(rot_sin[:, :, 1], sin))
            dve.sem_inc(setup_done, 1)

            def moments(n, p):
                dve.bn_stats(n.stats[:], x_of(p))
                dve.drain()
                dve.bn_aggr(n.moments[:], n.stats[:]).then_inc(n.moments_ready, 1)

            def normalize(n, turned, p):
                now(dve, n.rstd_ready, p)
                before(dve, turned, p)
                dve.tensor_scalar(n.normed[:], x_of(p), n.moments[:, 0:1], n.rstd[:], ALU.subtract, ALU.mult).then_inc(n.normed_ready, 1)

            def rotate(p):
                now(dve, A.qkv_ready, p)
                before(dve, A.rotated, p)
                qk = A.lin[:, 0:2 * D].rearrange("p (a n e) -> p a n e", a=2, e=2)
                n = D // 2
                full = [128, 2, n, 2]
                ra = rot_a[:].rearrange("p (a n) e -> p a n e", a=2)
                rb = rot_b[:].rearrange("p (a n) e -> p a n e", a=2)
                dve.tensor_tensor(ra.rearrange("p a n e -> p a (n e)"), A.lin[:, 0:2 * D].rearrange("p (a m) -> p a m", a=2),
                                  rot_cos[:].rearrange("p n e -> p (n e)").unsqueeze(1).broadcast_to([128, 2, D]), ALU.mult)
                for e in range(2):
                    last = dve.tensor_tensor(rb[:, :, :, e], qk[:, :, :, 1 - e],
                                             rot_sin[:, :, e].unsqueeze(1).broadcast_to([128, 2, n]), ALU.mult)
                last.then_inc(A.rotated_a, 1)

            def cross_low(p):
                now(dve, B.high_ready, p)
                now(dve, B.values_ready, p)
                q = B.lin[:, 0:D].rearrange("p (h d) -> p h d", d=DH)
                k = B.lin[:, D:2 * D].rearrange("p (h d) -> p h d", d=DH)
                dve.tensor_tensor(B.slots[:, 0, :, 16:24], q, B.slots[:, 0, :, 0:8], ALU.subtract)
                dve.tensor_tensor(B.slots[:, 1, :, 8:16], k, B.slots[:, 1, :, 0:8], ALU.subtract).then_inc(B.low_ready, 1)

            def take_stacked(s, p):
                now(dve, s.slots_turned, p)
                before(dve, s.scoresT_ready, p, 2)
                if p.n0 >= 2:
                    dve.wait_ge(s.diag_ready[p.u], p.half * 64)
                dve.tensor_copy(s.stacked[:, p.u].rearrange("p a n -> p (a n)"), s.lin.bitcast(F16)).then_inc(s.stacked_ready, 1)

            def maximum(s, p):
                now(dve, s.scores_ready, p)
                dve.tensor_reduce(s.neg_max[:], s.scores.rearrange("p b (h k) -> p (b h) k", k=SEQ), AX.X, ALU.max, negate=True).then_inc(s.max_ready, 1)
                now(dve, s.max_ready, p)
                dve.tensor_copy(s.max_parts[:, 0], s.neg_max[:]).then_inc(s.max_high_ready, 1)
                now(dve, s.max_high_ready, p)
                dve.tensor_tensor(s.max_parts[:, 1], s.neg_max[:], s.max_parts[:, 0], ALU.subtract).then_inc(s.max_split, 1)

            def divide(s, p):
                now(dve, s.mixed_ready, p)
                dve.reciprocal(s.inv_sum[:], s.scores[:, 0, TOK:2 * TOK]).then_inc(s.inv_sum_ready, 1)
                now(dve, s.inv_sum_ready, p)
                dve.tensor_tensor(s.mixedT[:], s.scores[:, 0, 0:TOK], s.inv_sum[:], ALU.mult).then_inc(s.mixedT_ready, 1)

            def add_residual(s, p):
                now(dve, s.projected, p)
                dve.tensor_tensor(x_of(p), s.scores[:, 1, 0:D], x_of(p), ALU.add).then_inc(s.x_updated, 1)

            def ffn_gated(p):
                now(dve, F.tanh_ready, p)
                dve.scalar_tensor_tensor(F.gated[:], F.tanh[:], 1.0, F.gate[:, 0:HIDDEN], ALU.add, ALU.mult).then_inc(F.gated_ready, 1)
                now(dve, F.gated_ready, p)
                before(dve, F.down_ready, p)
                dve.scalar_tensor_tensor(F.hidden[:], F.up[:, 0:HIDDEN], 0.5 * DEQUANT * DEQUANT, F.gated[:], ALU.mult, ALU.mult).then_inc(F.hidden_ready, 1)

            def ffn_residual(p):
                now(dve, F.down_ready, p)
                dve.scalar_tensor_tensor(x_of(p), F.gate[:, 0:D], DEQUANT, x_of(p), ALU.mult, ALU.add).then_inc(F.x_updated, 1)

            def step(pair):
                a0, a1, b0, b1, f = (pair(s) for s in range(5))
                if a0.live:
                    if a0.n0 == 0:
                        dve.wait_ge(x_first_loaded, 16)
                    if a0.n0 == 4:
                        dve.wait_ge(x_rest_loaded, 16)
                    moments(A.norm, a0)
                if b0.live:
                    dve.wait_ge(x_first_loaded, 16)
                    now(dve, A.x_updated, b0)
                    moments(B.norm, b0)
                if f.live:
                    dve.wait_ge(x_first_loaded, 16)
                    now(dve, B.x_updated, f)
                    moments(F.norm, f)
                if a0.live:
                    normalize(A.norm, A.inputs_turned, a0)
                if b0.live:
                    normalize(B.norm, B.inputs_turned, b0)
                if f.live:
                    normalize(F.norm, F.input_turned, f)
                if a1.live:
                    maximum(A, a1)
                if b1.live:
                    maximum(B, b1)
                if a0.live:
                    rotate(a0)
                if b0.live:
                    cross_low(b0)
                if f.live:
                    ffn_gated(f)
                if a0.live:
                    take_stacked(A, a0)
                if b0.live:
                    take_stacked(B, b0)
                if a1.live:
                    divide(A, a1)
                if b1.live:
                    divide(B, b1)
                if a1.live:
                    add_residual(A, a1)
                if f.live:
                    ffn_residual(f)
                if b1.live:
                    add_residual(B, b1)

            run(dve, step)

        @block.tensor
        def _(pe):
            pe.wait_ge(const_loaded, 16 * N_CONST)
            pe.wait_ge(setup_done, 1)
            pe.wait_ge(slots_cleared, 1)

            def mm(o, lhsT, rhs, start):
                return pe.matmul(o, lhsT, rhs, start=start, stop=True, skip_group_check=True)

            def turn_self(p):
                now(pe, A.norm.normed_ready, p)
                before(pe, A.stacked_ready, p)
                pe.transpose(A.lin[:, 0:TOK], A.norm.normed[:], ident[:]).then_inc(A.inputs_turned, 1)

            def turn_cross(p):
                now(pe, B.norm.normed_ready, p)
                before(pe, B.stacked_ready, p)
                pe.wait_ge(context_loaded[p.u], p.half * 16 + 16)
                pe.transpose(B.lin[:, 0:TOK], B.norm.normed[:], ident[:])
                pe.transpose(B.lin[:, TOK:2 * TOK], context[:, p.u, :], ident[:]).then_inc(B.inputs_turned, 1)

            def turn_ffn(p):
                now(pe, F.norm.normed_ready, p)
                before(pe, F.x_updated, p)
                pe.transpose(F.gate[:, 0:TOK], F.norm.normed[:], ident[:]).then_inc(F.input_turned, 1)

            def project_values(s, source, w, start):
                for b in range(2):
                    for half in range(2):
                        last = mm(s.lin[SEQ * half:SEQ * (half + 1), (2 + b) * D:(3 + b) * D],
                                  source[:, SEQ * b:SEQ * (b + 1)], w[:, 2 * D:3 * D], start)
                last.then_inc(s.qkv_ready, 1)

            def self_qkv(p):
                now(pe, A.inputsT_ready, p)
                mm(A.lin[:, 0:2 * D], A.inputsT[:, 0, :], w_self[:, 0:2 * D], True)
                project_values(A, A.inputsT[:, 0, :], w_self, True)

            def cross_qkv(p):
                now(pe, B.inputsT_ready, p)
                mm(B.lin, one_rows[:], bias_parts[:, 0:4 * D], True)
                mm(B.lin[:, 0:D], B.inputsT[:, 0, :], w_cross[:, 0:D], False)
                mm(B.lin[:, D:2 * D], B.inputsT[:, 1, :], w_cross[:, D:2 * D], False)
                project_values(B, B.inputsT[:, 1, :], w_cross, False)

            def turn_slots(s, p):
                now(pe, s.low_ready, p)
                now(pe, s.values_ready, p)
                turned = s.lin.bitcast(F16)
                for n in range(2):
                    for g in range(GROUPS):
                        at = (n * GROUPS + g) * TOK
                        last = pe.transpose(turned[:, at:at + TOK], s.slots[:, n, 4 * g:4 * g + 4, :].rearrange("p h s -> p (h s)"), ident16[:])
                last.then_inc(s.slots_turned, 1)

            def scores(s, p):
                pe.wait_ge(s.diag_ready[p.u], p.half * 64 + 64)
                before(pe, s.x_updated, p)
                if s.causal:
                    for n in range(2):
                        mm(s.scores[:, n, :], future[:], key_is[:], True)
                for g in range(GROUPS):
                    for b in range(2):
                        cols = slice(g * TOK + b * SEQ, g * TOK + (b + 1) * SEQ)
                        last = mm(s.scores[SEQ * b:SEQ * (b + 1), g // 2, 256 * (g % 2):256 * (g % 2 + 1)],
                                  s.stacked[:, p.u, 0, cols], s.key_diag[:, p.u, 2 * g + b].rearrange("p h k -> p (h k)"), not s.causal and g % 2 == 0)
                last.then_inc(s.scores_ready, 1)

            def scoresT_bank(s, p, n):
                for m in range(4):
                    hp = 4 * n + m
                    for b in range(2):
                        cols = slice(hp // 2 * TOK + b * SEQ, hp // 2 * TOK + (b + 1) * SEQ)
                        mm(s.scores[:, n, m * TOK + b * SEQ:m * TOK + (b + 1) * SEQ],
                           s.key_diag[:, p.u, hp // 2 * 2 + b, 2 * (hp % 2):2 * (hp % 2) + 2].rearrange("p h k -> p (h k)"), s.stacked[:, p.u, 0, cols],
                           m == 0 and b == 0)

            def turn_max(s, p):
                now(pe, s.max_split, p)
                pe.transpose(s.scores[0:2 * HEADS, 1, 0:TOK // 2].bitcast(BF16), s.max_parts[:].rearrange("p a h -> p (a h)"), identb[:]).then_inc(s.max_turned, 1)

            def scoresT(s, p):
                scoresT_bank(s, p, 0)
                now(pe, s.shift_ready, p)
                scoresT_bank(s, p, 1)
                for hp in range(HPAIRS):
                    last = mm(s.scores[:, hp // 4, (hp % 4) * TOK:(hp % 4 + 1) * TOK], shift_pick[:, hp, :], s.shift[:], False)
                last.then_inc(s.scoresT_ready, 1)

            def mix(s, p):
                now(pe, s.probs_ready, p)
                for i in range(2):
                    for j in range(4):
                        hp = 2 * j + i
                        mm(s.scores[32 * j:32 * j + 32, 0, TOK:2 * TOK], ones[:, i, :], s.probs[:, hp * TOK:(hp + 1) * TOK], i == 0)
                for i in range(2):
                    for b in range(2):
                        for j in range(4):
                            hp = 2 * j + i
                            v = s.values[:, p.u, 4 * b + j, 2 * i:2 * i + 2, :].rearrange("p c d -> p (c d)")
                            last = mm(s.scores[32 * j:32 * j + 32, 0, SEQ * b:SEQ * (b + 1)], v,
                                      s.probs[:, hp * TOK + b * SEQ:hp * TOK + (b + 1) * SEQ], False)
                last.then_inc(s.mixed_ready, 1)

            def project(s, w, p):
                now(pe, s.mixedT_ready, p)
                if not s.causal:
                    mm(s.scores[:, 1, 0:D], one_rows[:], bias_parts[:, 4 * D:5 * D], True)
                mm(s.scores[:, 1, 0:D], s.mixedT[:], w[:], s.causal).then_inc(s.projected, 1)

            def gate_up(p):
                now(pe, F.inputT_ready, p)
                before(pe, F.hidden_ready, p)
                for n, bank in ((0, F.gate), (1, F.up)):
                    for c in range(CHUNKS):
                        last = mm(bank[:, c * TOK:(c + 1) * TOK], w_ffn[:, n, c * 128:(c + 1) * 128], F.inputT[:], True)
                last.then_inc(F.gate_up_ready, 1)

            def down(p):
                now(pe, F.hidden_ready, p)
                for c in range(CHUNKS):
                    last = mm(F.gate[:, 0:D], F.hidden[:, c * TOK:(c + 1) * TOK], w_ffn[:, 2, c * D:(c + 1) * D], c == 0)
                last.then_inc(F.down_ready, 1)

            def step(pair):
                a0, a1, b0, b1, f = (pair(s) for s in range(5))
                if a1.live:
                    scores(A, a1)
                if a0.live:
                    turn_self(a0)
                if b0.live:
                    turn_cross(b0)
                if f.live:
                    turn_ffn(f)
                if b1.live:
                    scores(B, b1)
                if a0.live:
                    self_qkv(a0)
                if a1.live:
                    turn_max(A, a1)
                if b0.live:
                    cross_qkv(b0)
                if a1.live:
                    scoresT(A, a1)
                if f.live:
                    gate_up(f)
                if b1.live:
                    turn_max(B, b1)
                if a0.live:
                    turn_slots(A, a0)
                if b1.live:
                    scoresT(B, b1)
                if b0.live:
                    turn_slots(B, b0)
                if a1.live:
                    mix(A, a1)
                if b1.live:
                    mix(B, b1)
                if f.live:
                    down(f)
                if a1.live:
                    project(A, w_self_out, a1)
                if b1.live:
                    project(B, w_cross_out, b1)

            run(pe, step)


def kernel(**inputs):
    import numpy as _np
    import concourse.bacc as _bacc
    from concourse import mybir as _mybir
    from concourse.bass_utils import run_bass_kernel_spmd as _run

    def flat(name):
        return _np.ascontiguousarray(_np.asarray(inputs[name]).reshape(-1, D))

    def turned(name):
        return _np.ascontiguousarray(_np.asarray(inputs[name]).T)

    def row(name):
        return _np.ascontiguousarray(_np.asarray(inputs[name]))

    arrays = {
        "x": flat("x"), "ctx": flat("ctx_1024"),
        "w_qkvT": turned("L0_attn_Wqkv"), "w_self_outT": turned("L0_attn_Wo"),
        "log_xi": row("L0_attn_log_xi"), "pi_gate": row("L0_attn_pi_gate_logit"), "e_gate": row("L0_attn_e_gate_logit"),
        "w_qT": turned("L0_xattn_W_q"), "w_kT": turned("L0_xattn_W_k"), "w_vT": turned("L0_xattn_W_v"),
        "w_cross_outT": turned("L0_xattn_W_o"),
        "b_q": row("L0_xattn_b_q"), "b_k": row("L0_xattn_b_k"), "b_v": row("L0_xattn_b_v"), "b_o": row("L0_xattn_b_o"),
        "w_gateT": turned("L0_ffn_w_gate"), "w_upT": turned("L0_ffn_w_up"), "w_downT": turned("L0_ffn_w_down"),
        **constants(),
    }
    nc = _bacc.Bacc("TRN2", target_bir_lowering=False, num_devices=1)
    aps = {n: nc.dram_tensor(f"in_{n}", v.shape, _mybir.dt.from_np(v.dtype), kind="ExternalInput").ap() for n, v in arrays.items()}
    out = nc.dram_tensor("out_x", (BATCH * SEQ, D), F32, kind="ExternalOutput").ap()
    aps["out_flat"] = out
    build(nc, aps, out)
    r = _run(nc, [{f"in_{n}": v for n, v in arrays.items()}], core_ids=[0])
    return _np.asarray(r.results[0]["out_x"]).reshape(BATCH, SEQ, D)
```

```python
from contextlib import ExitStack

import numpy as np
import concourse.bass as bass
from concourse import mybir

F32 = mybir.dt.float32
F16 = mybir.dt.float16
BF16 = mybir.dt.bfloat16
I32 = mybir.dt.int32
ALU = mybir.AluOpType
ACT = mybir.ActivationFunctionType
AX = mybir.AxisListType

BATCH, SEQ, D = 128, 64, 128
HEADS, DH = 16, 8
HIDDEN = 384
CHUNKS = HIDDEN // 128
TOK = 2 * SEQ
PAIRS = BATCH * SEQ // TOK
SLOT = 32
GROUPS = HEADS * SLOT // 128
HPAIRS = HEADS // 2
EPS = 1e-5
SCORE_SCALE = float(DH) ** -0.5
DEQUANT = 1.0 / 127.0
W_SCALE = 16.0
MASKED = -1e30
MAX_DECAY = 336.0
SHIFT_ROWS = 2 * HEADS + SEQ
LAG_CROSS = 3
LAG_FFN = 7
LAST_LAG = 8
UNROLL = 4
PEELED = LAST_LAG + 2
PEELED += (PAIRS - PEELED) % UNROLL
assert PEELED % 2 == 0 and UNROLL % 2 == 0
TWO_PI = 2 * np.pi
TWO_PI_HIGH = 6.28125
ROUND = 1.5 * 2.0 ** 23


class Indices:
    def __init__(self, eng, i):
        self.eng, self.i, self.known = eng, i, {}

    def __getitem__(self, n):
        if n not in self.known:
            register = self.eng.alloc_register(f"index_{n}")
            self.eng.reg_mov(register, UNROLL * self.i + n)
            self.known[n] = self.eng.snap(register, min_val=n, max_val=PAIRS - PEELED - UNROLL + n)
        return self.known[n]


class Record:
    pass


def constants():
    tok = np.arange(TOK)
    k = tok % SEQ
    bf = mybir.dt.np(BF16)
    future = np.where(np.arange(SEQ)[:, None] > k[None, :], MASKED, 0.0)
    shift_pick = np.zeros((SHIFT_ROWS, HPAIRS, 2, SEQ), np.float32)
    for h in range(HEADS):
        shift_pick[2 * h:2 * h + 2, h // 2, h % 2] = 1
    for j in range(SEQ):
        shift_pick[2 * HEADS + j, :, :, j] = 1
    ones = np.zeros((2, SEQ, 2, 4, DH), np.float32)
    for h2 in range(2):
        for i in range(2):
            ones[h2, :, i, 2 * i + h2] = 1
    freq = np.float32(np.pi) ** (np.float32(1) - np.arange(0, DH, 2, dtype=np.float32) / np.float32(DH))
    return {
        "c_ident": np.eye(128, dtype=np.float32),
        "c_ident16": np.eye(128, dtype=np.float16),
        "c_identb": np.eye(128).astype(bf),
        "c_future": future.astype(bf),
        "c_key_is": np.tile(np.eye(SEQ), (1, 8)).astype(bf),
        "c_shift_pick": shift_pick.reshape(SHIFT_ROWS, HPAIRS * 128).astype(bf),
        "c_ones": ones.reshape(128, 2 * 4 * DH),
        "c_angle": (k[:, None].astype(np.float32) * freq[None, :].astype(np.float32)),
        "c_kpos": k[:, None].astype(np.float32),
        "c_part": np.eye(3, dtype=np.float32),
    }


def build(nc, a, out):
    x_d = a["x"].rearrange("(p t) d -> t p d", t=TOK)
    out_d = out.rearrange("(p t) d -> t p d", t=TOK)

    with ExitStack() as ctx:
        def sb(name, shape, dt=F32):
            return ctx.enter_context(nc.sbuf_tensor(name, shape, dt))

        def sem(name):
            return ctx.enter_context(nc.semaphore(name))

        psum = ctx.enter_context(nc.psum_tensor("psum", [128, 8, 512], F32))

        ident = sb("ident", [128, 128])
        ident16 = sb("ident16", [128, 128], F16)
        identb = sb("identb", [128, 128], BF16)
        future = sb("future", [SEQ, TOK], BF16)
        key_is = sb("key_is", [SEQ, 512], BF16)
        shift_pick = sb("shift_pick", [SHIFT_ROWS, HPAIRS, 128], BF16)
        ones = sb("ones", [128, 2, 4 * DH])
        angle = sb("angle", [128, DH // 2])
        kpos = sb("kpos", [128, 1])
        part = sb("part", [3, 3])
        w_self = sb("w_self", [128, 3 * D])
        w_self16 = sb("w_self16", [128, 2, 3 * D], F16)
        w_cross16 = sb("w_cross16", [128, 2, 3 * D], F16)
        w_self_out = sb("w_self_out", [128, D])
        w_cross = sb("w_cross", [128, 3 * D])
        w_cross_out = sb("w_cross_out", [128, D])
        w_int = sb("w_int", [128, 3, HIDDEN], I32)
        w_in = sb("w_in", [128, 2, HIDDEN], F16)
        w_down = sb("w_down", [128, HIDDEN], F16)
        gates = sb("gates", [128, 3, HEADS])
        biases = sb("biases", [3, 5 * D])
        bias_rest = sb("bias_rest", [3, 5 * D])
        bias_cut = sb("bias_cut", [3, 3, 5 * D], BF16)
        bias_sum = sb("bias_sum", [3, 2, 5 * D])
        bias_parts = sb("bias_parts", [3, 5 * D], BF16)
        one_rows = sb("one_rows", [3, TOK], BF16)
        minus_half = sb("minus_half", [128, 1])
        eps = sb("eps", [128, 1])
        one = sb("one", [128, 1])

        gate_tanh = sb("gate_tanh", [128, 3, HEADS])
        gate = sb("gate", [128, 3, HEADS])
        inv_xi = sb("inv_xi", [128, HEADS])
        theta = sb("theta", [128, HEADS, DH // 2])
        turns = sb("turns", [128, 2, HEADS, DH // 2])
        reduced = sb("reduced", [128, 2, HEADS, DH // 2])
        sincos = sb("sincos", [128, 2, HEADS, DH // 2])
        rot_cos = sb("rot_cos", [128, HEADS * DH // 2, 2])
        rot_sin = sb("rot_sin", [128, HEADS * DH // 2, 2])
        decay = sb("decay", [128, HEADS])
        decay_rest = sb("decay_rest", [128, 2, HEADS])

        x_all = sb("x_all", [128, PAIRS * D])
        context = sb("context", [128, 2, D])

        const_loaded = sem("const_loaded")
        x_first_loaded = sem("x_first_loaded")
        x_rest_loaded = sem("x_rest_loaded")
        slots_cleared = sem("slots_cleared")
        dve_setup = sem("dve_setup")
        act_setup = sem("act_setup")
        angles_ready = sem("angles_ready")
        setup_done = sem("setup_done")
        context_loaded = [sem(f"context_loaded{u}") for u in range(2)]
        stored = sem("stored")

        stats = sb("stats", [128, 3, 6])
        moments = sb("moments", [128, 3, 2])
        var_eps = sb("var_eps", [128, 3])
        rstd = sb("rstd", [128, 3])
        moments_ready = sem("moments_ready")
        var_ready = sem("var_ready")
        rstd_ready = sem("rstd_ready")
        split_high = [sem(f"{n}_input_high") for n in ("self", "cross", "ffn", "context")]
        split_done = [sem(f"{n}_input_split") for n in ("self", "cross", "ffn", "context")]
        normed_ready = [sem(f"{n}_normed_ready") for n in ("self", "cross", "ffn")]
        normed = [sb(f"{n}_normed", [128, D]) for n in ("self", "cross", "ffn")]
        split = [sb(f"{n}_split", [128, 2, D], F16) for n in ("self", "cross", "ffn", "context")]

        def attention_state(n, bank, score_bank):
            s = Record()
            s.causal = n == "self"
            s.lin, s.scores = psum[:, bank, :], psum[:, score_bank:score_bank + 2, :]
            s.inputsT = sb(f"{n}_inputsT", [128, 2, 2, TOK], F16)
            s.slots = sb(f"{n}_slots", [128, 2, HEADS, SLOT], F16)
            s.stacked = sb(f"{n}_stacked", [128, 2, 2, GROUPS * TOK], F16)
            s.key_diag = sb(f"{n}_key_diag", [128, 2, 2 * GROUPS, 4, SEQ], F16)
            s.values = sb(f"{n}_values", [128, 2, 8, 4, 2 * DH])
            s.neg_max = sb(f"{n}_neg_max", [128, HEADS])
            s.shift = sb(f"{n}_shift", [SHIFT_ROWS, TOK], BF16)
            s.probs = sb(f"{n}_probs", [128, HPAIRS * TOK])
            s.inv_sum = sb(f"{n}_inv_sum", [128, TOK])
            s.mixedT = sb(f"{n}_mixedT", [128, TOK])
            s.inputs_turned = sem(f"{n}_inputs_turned")
            s.inputsT_ready = sem(f"{n}_inputsT_ready")
            s.qkv_ready = sem(f"{n}_qkv_ready")
            s.rotated_a = sem(f"{n}_rotated_a")
            s.rotated = sem(f"{n}_rotated")
            s.high_ready = sem(f"{n}_high_ready")
            s.values_ready = sem(f"{n}_values_ready")
            s.low_ready = sem(f"{n}_low_ready")
            s.slots_turned = sem(f"{n}_slots_turned")
            s.stacked_ready = sem(f"{n}_stacked_ready")
            s.scores_ready = sem(f"{n}_scores_ready")
            s.max_ready = sem(f"{n}_max_ready")
            s.max_split = sem(f"{n}_max_split")
            s.max_turned = sem(f"{n}_max_turned")
            s.shift_ready = sem(f"{n}_shift_ready")
            s.scoresT_ready = sem(f"{n}_scoresT_ready")
            s.probs_ready = sem(f"{n}_probs_ready")
            s.mixed_ready = sem(f"{n}_mixed_ready")
            s.inv_sum_ready = sem(f"{n}_inv_sum_ready")
            s.mixedT_ready = sem(f"{n}_mixedT_ready")
            s.projected = sem(f"{n}_projected")
            s.x_updated = sem(f"{n}_x_updated")
            s.diag_ready = [sem(f"{n}_diag_ready{u}") for u in range(2)]
            return s

        A = attention_state("self", 4, 0)
        B = attention_state("cross", 5, 2)
        rot_a = sb("rot_a", [128, 2 * D // 2, 2])
        rot_b = sb("rot_b", [128, 2 * D // 2, 2])
        rot = sb("rot", [128, 2, HEADS, DH])
        cross_qk = sb("cross_qk", [128, 2, HEADS, DH])
        F = Record()
        F.gate, F.up = psum[:, 6, :], psum[:, 7, :]
        F.inputT = sb("ffn_inputT", [128, 2, TOK], F16)
        F.tanh = sb("ffn_tanh", [128, HIDDEN])
        F.gated = sb("ffn_gated", [128, HIDDEN])
        F.hidden = sb("ffn_hidden", [128, HIDDEN])
        F.hidden16 = sb("ffn_hidden16", [128, 2, HIDDEN], F16)
        F.input_turned = sem("ffn_input_turned")
        F.inputT_ready = sem("ffn_inputT_ready")
        F.gate_up_ready = sem("ffn_gate_up_ready")
        F.tanh_ready = sem("ffn_tanh_ready")
        F.gated_ready = sem("ffn_gated_ready")
        F.hidden_ready = sem("ffn_hidden_ready")
        F.hidden_high = sem("ffn_hidden_high")
        F.hidden_low = sem("ffn_hidden_low")
        F.down_ready = sem("ffn_down_ready")
        F.x_updated = sem("ffn_x_updated")

        def pair_at(n0, i, counts):
            p = Record()
            p.first = n0
            p.u = n0 % 2
            p.live = i is not None or 0 <= n0 < PAIRS
            p.half = n0 // 2 if i is None else n0 // 2 + UNROLL // 2 * i
            p.counts = counts
            p.loop = i
            return p

        def index(p, ahead=0):
            return p.first + ahead if p.counts is None else p.counts[p.first + ahead]

        def later(p, n):
            return pair_at(p.first + n, p.loop, p.counts)

        def for_live_pairs(work):
            def guarded(*args):
                if args[-1].live:
                    work(*args)
            return guarded

        def run(eng, step):
            for t in range(PEELED):
                step(lambda lag: pair_at(t - lag, None, None))
            with eng.Fori(0, (PAIRS - PEELED) // UNROLL) as i:
                indices = Indices(eng, i)
                for t in range(PEELED, PEELED + UNROLL):
                    step(lambda lag: pair_at(t - lag, i, indices))
            for t in range(PAIRS, PAIRS + LAST_LAG):
                step(lambda lag: pair_at(t - lag, None, None))

        def x_of(p):
            return x_all[:, bass.ds(index(p) * D, D)]

        block = ctx.enter_context(nc.Block())

        N_CONST = 27
        @block.sync
        def _(sp):
            for dst, src in (
                    (gates[:, 0, :], a["log_xi"].partition_broadcast(128)),
                    (gates[:, 1, :], a["pi_gate"].partition_broadcast(128)),
                    (gates[:, 2, :], a["e_gate"].partition_broadcast(128)),
                    (angle[:], a["c_angle"]), (kpos[:], a["c_kpos"]), (part[:], a["c_part"]),
                    (ident[:], a["c_ident"]), (ident16[:], a["c_ident16"]), (identb[:], a["c_identb"]),
                    (future[:], a["c_future"]), (key_is[:], a["c_key_is"]),
                    (shift_pick[:].rearrange("p a b -> p (a b)"), a["c_shift_pick"]),
                    (ones[:].rearrange("p a b -> p (a b)"), a["c_ones"]),
                    (w_self[:], a["w_qkvT"]), (w_self_out[:], a["w_self_outT"]),
                    (w_cross[:, 0:D], a["w_qT"]), (w_cross[:, D:2 * D], a["w_kT"]),
                    (w_cross[:, 2 * D:3 * D], a["w_vT"]), (w_cross_out[:], a["w_cross_outT"]),
                    (w_int[:, 0, :], a["w_gateT"]), (w_int[:, 1, :], a["w_upT"]),
                    (w_int[:, 2, :].rearrange("p (c d) -> p c d", c=CHUNKS),
                     a["w_downT"].rearrange("(c p) d -> p c d", c=CHUNKS)),
                    (biases[:, 0:D], a["b_q"].partition_broadcast(3)),
                    (biases[:, D:2 * D], a["b_k"].partition_broadcast(3)),
                    (biases[:, 2 * D:3 * D], a["b_v"].partition_broadcast(3)),
                    (biases[:, 3 * D:4 * D], a["b_v"].partition_broadcast(3)),
                    (biases[:, 4 * D:5 * D], a["b_o"].partition_broadcast(3))):
                sp.dma_start(dst, src).then_inc(const_loaded, 16)

            @for_live_pairs
            def load_context(p):
                if p.first >= 2:
                    sp.wait_ge(split_done[3], index(p, -1))
                sp.dma_start(context[:, p.u, :], a["ctx"][bass.ds(index(p) * TOK, TOK), :]).then_inc(context_loaded[p.u], 16)

            @for_live_pairs
            def spread_keys(s, p):
                if p.first >= 2:
                    sp.wait_ge(s.scoresT_ready, index(p, -1))
                sp.wait_ge(s.stacked_ready, index(p, 1))
                for h in range(4):
                    rows = slice(SLOT * h, SLOT * (h + 1))
                    sp.dma_start(s.key_diag[rows, p.u, :, h, :], s.stacked[rows, p.u, 1, :].rearrange("p (n k) -> p n k", k=SEQ)).then_inc(s.diag_ready[p.u], 16)

            @for_live_pairs
            def store(p):
                rows = a["out_flat"][bass.ds(index(p) * TOK, TOK), :]
                sp.wait_ge(F.x_updated, index(p, 1))
                sp.dma_start(rows, x_of(p)).then_inc(stored, 16)

            sp.wait_ge(slots_cleared, 1)

            def step(at):
                spread_keys(A, at(0))
                load_context(at(0))
                spread_keys(B, at(2))
                store(at(7))

            run(sp, step)
            sp.wait_ge(stored, 16 * PAIRS)

        @block.gpsimd
        def _(pool):
            pool.memset(minus_half[:], -0.5)
            pool.memset(eps[:], EPS)
            pool.memset(one[:], 1.0)
            pool.memset(A.values[:], 0.0)
            pool.memset(B.values[:], 0.0)
            pool.memset(A.key_diag[:], 0.0)
            pool.memset(B.key_diag[:], 0.0).then_inc(slots_cleared, 1)
            pool.wait_ge(slots_cleared, 1)

            def inverse_deviation(t):
                pool.wait_ge(moments_ready, index(t, 1))
                pool.tensor_tensor(var_eps[:], moments[:, :, 1], eps[:].broadcast_to([128, 3]), ALU.add).then_inc(var_ready, 1)
                pool.wait_ge(var_ready, index(t, 1))
                pool.tensor_tensor(rstd[:], var_eps[:], minus_half[:].broadcast_to([128, 3]), ALU.pow).then_inc(rstd_ready, 1)

            @for_live_pairs
            def add_rotation(p):
                pool.wait_ge(A.rotated_a, index(p, 1))
                if p.first >= 1:
                    pool.wait_ge(A.high_ready, index(p))
                if p.first >= 1:
                    pool.wait_ge(A.low_ready, index(p))
                pool.tensor_tensor(rot[:].rearrange("p a h d -> p (a h d)"), rot_a[:].rearrange("p a b -> p (a b)"),
                                   rot_b[:].rearrange("p a b -> p (a b)"), ALU.add).then_inc(A.rotated, 1)

            @for_live_pairs
            def split_low(p):
                pool.wait_ge(A.high_ready, index(p, 1))
                pool.tensor_tensor(A.slots[:, 0, :, 16:24], rot[:, 0], A.slots[:, 0, :, 0:8], ALU.subtract)
                pool.tensor_tensor(A.slots[:, 1, :, 8:16], rot[:, 1], A.slots[:, 1, :, 0:8], ALU.subtract).then_inc(A.low_ready, 1)

            def split_input(n, source, turned, p):
                if p.first >= 1:
                    pool.wait_ge(turned, index(p))
                pool.tensor_tensor(split[n][:, 0], source, one[:].broadcast_to([128, D]), ALU.mult).then_inc(split_high[n], 1)
                pool.wait_ge(split_high[n], index(p, 1))
                pool.tensor_tensor(split[n][:, 1], source, split[n][:, 0], ALU.subtract).then_inc(split_done[n], 1)

            @for_live_pairs
            def split_self(p):
                pool.wait_ge(normed_ready[0], index(p, 1))
                split_input(0, normed[0][:], A.inputs_turned, p)

            @for_live_pairs
            def split_cross(p):
                pool.wait_ge(normed_ready[1], index(p, 1))
                split_input(1, normed[1][:], B.inputs_turned, p)

            @for_live_pairs
            def split_ffn(p):
                pool.wait_ge(normed_ready[2], index(p, 1))
                split_input(2, normed[2][:], F.input_turned, p)

            @for_live_pairs
            def split_context(p):
                pool.wait_ge(context_loaded[p.u], p.half * 16 + 16)
                split_input(3, context[:, p.u, :], B.inputs_turned, p)

            @for_live_pairs
            def cross_low(p):
                pool.wait_ge(B.high_ready, index(p, 1))
                pool.tensor_tensor(B.slots[:, 0, :, 16:24], cross_qk[:, 0], B.slots[:, 0, :, 0:8], ALU.subtract)
                pool.tensor_tensor(B.slots[:, 1, :, 8:16], cross_qk[:, 1], B.slots[:, 1, :, 0:8], ALU.subtract).then_inc(B.low_ready, 1)

            @for_live_pairs
            def hidden_low(p):
                pool.wait_ge(F.hidden_high, index(p, 1))
                pool.tensor_tensor(F.hidden16[:, 1], F.hidden[:], F.hidden16[:, 0], ALU.subtract).then_inc(F.hidden_low, 1)

            def step(at):
                split_low(at(1))
                inverse_deviation(at(0))
                split_cross(at(3))
                split_self(at(0))
                hidden_low(at(8))
                split_ffn(at(7))
                cross_low(at(3))
                add_rotation(at(0))
                split_context(at(2))

            run(pool, step)

        @block.scalar
        def _(act):
            act.dma_start(x_all[:, 0:4 * D].rearrange("t (p d) -> t p d", d=D), x_d[:, 0:4, :]).then_inc(x_first_loaded, 16)
            act.dma_start(x_all[:, 4 * D:].rearrange("t (p d) -> t p d", d=D), x_d[:, 4:PAIRS, :]).then_inc(x_rest_loaded, 16)
            act.wait_ge(const_loaded, 16 * N_CONST)
            act.activation(inv_xi[:], gates[:, 0, :], ACT.Exp, scale=-1.0)
            act.activation(gate_tanh[:], gates[:], ACT.Tanh, scale=0.5).then_inc(act_setup, 1)
            act.wait_ge(angles_ready, 1)
            act.activation(sincos[:], reduced[:], ACT.Sin).then_inc(act_setup, 1)
            act.wait_ge(setup_done, 1)

            @for_live_pairs
            def turn_self_in(p):
                act.wait_ge(A.inputs_turned, index(p, 1))
                act.activation(A.inputsT[:, 0].rearrange("p a t -> p (a t)"), A.lin[:, 0:TOK].bitcast(F16), ACT.Copy).then_inc(A.inputsT_ready, 1)

            @for_live_pairs
            def turn_cross_in(p):
                act.wait_ge(B.inputs_turned, index(p, 1))
                act.activation(B.inputsT[:].rearrange("p n a t -> p (n a t)"), B.lin[:, 0:2 * TOK].bitcast(F16), ACT.Copy).then_inc(B.inputsT_ready, 1)

            @for_live_pairs
            def turn_ffn_in(p):
                act.wait_ge(F.input_turned, index(p, 1))
                act.activation(F.inputT[:].rearrange("p a t -> p (a t)"), F.gate[:, 0:TOK].bitcast(F16), ACT.Copy).then_inc(F.inputT_ready, 1)

            def high_parts(s, q, k):
                act.activation(s.slots[:, 0, :, 0:16].rearrange("p h (r d) -> p h r d", d=DH),
                               q.unsqueeze(2).broadcast_to([128, HEADS, 2, DH]), ACT.Copy)
                act.activation(s.slots[:, 1, :, 0:8], k, ACT.Copy)
                act.activation(s.slots[:, 1, :, 16:24], k, ACT.Copy).then_inc(s.high_ready, 1)

            @for_live_pairs
            def take_values(s, p):
                if p.first >= 2:
                    act.wait_ge(s.mixed_ready, index(p, -1))
                v = s.lin[:, 2 * D:3 * D].rearrange("p (j i t d) -> p j i t d", i=2, t=2, d=DH)
                for b in range(2):
                    for t in range(2):
                        last = act.activation(s.values[SEQ * t:SEQ * (t + 1), p.u, 4 * b:4 * b + 4, 0:4:3, t * DH:(t + 1) * DH],
                                              v[SEQ * b:SEQ * (b + 1), :, :, t, :], ACT.Copy, scale=1 / W_SCALE)
                last.then_inc(s.values_ready, 1)

            def heads(ap):
                return ap.rearrange("p (h d) -> p h d", d=DH)

            @for_live_pairs
            def self_values(p):
                act.wait_ge(A.rotated_a, index(p, 1))
                take_values(A, p)

            @for_live_pairs
            def self_high(p):
                act.wait_ge(A.rotated, index(p, 1))
                high_parts(A, rot[:, 0], rot[:, 1])

            @for_live_pairs
            def cross_high(p):
                act.wait_ge(B.qkv_ready, index(p, 1))
                act.activation(cross_qk[:].rearrange("p a h d -> p (a h d)"), B.lin[:, 0:2 * D], ACT.Copy)
                high_parts(B, heads(B.lin[:, 0:D]), heads(B.lin[:, D:2 * D]))

            @for_live_pairs
            def take_shift(s, p):
                act.wait_ge(s.max_turned, index(p, 1))
                if p.first >= 1:
                    act.wait_ge(s.scoresT_ready, index(p))
                turned = s.scores[0:2 * HEADS, 1, 0:TOK // 2].bitcast(BF16)
                act.activation(s.shift[0:2 * HEADS, :], turned, ACT.Copy).then_inc(s.shift_ready, 1)

            @for_live_pairs
            def exponent(s, p):
                act.wait_ge(s.scoresT_ready, index(p, 1))
                act.activation(s.probs[:].rearrange("p (b n) -> p b n", b=2), s.scores, ACT.Exp,
                               scale=SCORE_SCALE if s.causal else SCORE_SCALE / W_SCALE ** 2).then_inc(s.probs_ready, 1)

            @for_live_pairs
            def ffn_tanh(p):
                act.wait_ge(F.gate_up_ready, index(p, 1))
                if p.first >= 1:
                    act.wait_ge(F.gated_ready, index(p))
                act.activation(F.tanh[:], F.gate[:, 0:HIDDEN], ACT.Tanh, scale=0.5 * DEQUANT).then_inc(F.tanh_ready, 1)

            @for_live_pairs
            def hidden_high(p):
                act.wait_ge(F.hidden_ready, index(p, 1))
                if p.first >= 1:
                    act.wait_ge(F.down_ready, index(p))
                act.activation(F.hidden16[:, 0], F.hidden[:], ACT.Copy).then_inc(F.hidden_high, 1)

            @for_live_pairs
            def take_stacked(s, p):
                act.wait_ge(s.slots_turned, index(p, 1))
                if p.first >= 2:
                    act.wait_ge(s.scoresT_ready, index(p, -1))
                if p.first >= 2:
                    act.wait_ge(s.diag_ready[p.u], p.half * 64)
                act.activation(s.stacked[:, p.u].rearrange("p a n -> p (a n)"), s.lin.bitcast(F16), ACT.Copy).then_inc(s.stacked_ready, 1)

            def step(at):
                ffn_tanh(at(8))
                take_shift(A, at(2))
                exponent(B, at(5))
                exponent(A, at(2))
                take_stacked(A, at(1))
                hidden_high(at(8))
                turn_cross_in(at(3))
                turn_self_in(at(0))
                cross_high(at(3))
                take_values(B, at(3))
                self_values(at(0))
                turn_ffn_in(at(7))
                self_high(at(0))
                take_shift(B, at(4))
                take_stacked(B, at(3))

            run(act, step)

        @block.vector
        def _(dve):
            count = [0]

            def done(ins):
                ins.then_inc(dve_setup, 1)
                count[0] += 1
                dve.wait_ge(dve_setup, count[0])

            dve.wait_ge(act_setup, 1)
            done(dve.tensor_scalar(gate[:], gate_tanh[:], 0.5, 0.5, ALU.mult, ALU.add))
            done(dve.tensor_tensor(theta[:], angle[:].unsqueeze(1).broadcast_to([128, HEADS, DH // 2]),
                                   gate[:, 1, :].unsqueeze(2).broadcast_to([128, HEADS, DH // 2]), ALU.mult))
            dve.tensor_scalar(turns[:, 0], theta[:], 1 / TWO_PI, ROUND, ALU.mult, ALU.add)
            done(dve.tensor_scalar(turns[:, 1], theta[:], 1 / TWO_PI, 0.25, ALU.mult, ALU.add))
            done(dve.tensor_scalar(turns[:, 1], turns[:, 1], ROUND, None, ALU.add))
            done(dve.tensor_scalar(turns[:], turns[:], -ROUND, None, ALU.add))
            for n in range(2):
                last = dve.scalar_tensor_tensor(reduced[:, n], turns[:, n], -TWO_PI_HIGH, theta[:], ALU.mult, ALU.add)
            done(last)
            flat = reduced[:].rearrange("p a h i -> p (a h i)")
            done(dve.scalar_tensor_tensor(flat, turns[:].rearrange("p a h i -> p (a h i)"), -(TWO_PI - TWO_PI_HIGH), flat, ALU.mult, ALU.add))
            done(dve.tensor_scalar(reduced[:, 1], reduced[:, 1], np.pi / 2, None, ALU.add))
            dve.tensor_scalar(reduced[:], reduced[:], 3.1415925, -3.1415925, ALU.min, ALU.max).then_inc(angles_ready, 1)
            done(dve.tensor_tensor(decay[:], inv_xi[:], gate[:, 2, :], ALU.mult))
            done(dve.tensor_scalar(decay[:], decay[:], MAX_DECAY, 1 / SCORE_SCALE, ALU.min, ALU.mult))
            done(dve.tensor_scalar(decay[:], decay[:], kpos[:], None, ALU.mult))
            done(dve.memset(A.slots[:], 0.0))
            dve.memset(A.slots[:, 0, :, 24:27], 1.0)
            k1, k2, k3 = (A.slots[:, 1, :, n] for n in (24, 25, 26))
            done(dve.tensor_copy(k1, decay[:]))
            done(dve.tensor_tensor(decay_rest[:, 0], decay[:], k1, ALU.subtract))
            done(dve.tensor_copy(k2, decay_rest[:, 0]))
            done(dve.tensor_tensor(decay_rest[:, 1], decay_rest[:, 0], k2, ALU.subtract))
            dve.tensor_copy(k3, decay_rest[:, 1])
            dve.memset(B.slots[:], 0.0)
            for w16, w in ((w_self16, w_self), (w_cross16, w_cross)):
                done(dve.tensor_scalar(w16[:, 0], w[:], W_SCALE, None, ALU.mult))
                dve.scalar_tensor_tensor(w16[:, 1], w[:], W_SCALE, w16[:, 0], ALU.mult, ALU.subtract)
            done(dve.tensor_scalar(biases[:, 0:3 * D], biases[:, 0:3 * D], W_SCALE, None, ALU.mult))
            done(dve.tensor_copy(bias_cut[:, 0], biases[:]))
            done(dve.tensor_tensor(bias_rest[:], biases[:], bias_cut[:, 0], ALU.subtract))
            done(dve.tensor_copy(bias_cut[:, 1], bias_rest[:]))
            done(dve.tensor_tensor(bias_rest[:], bias_rest[:], bias_cut[:, 1], ALU.subtract))
            done(dve.tensor_copy(bias_cut[:, 2], bias_rest[:]))
            done(dve.tensor_scalar(bias_sum[:, 0], bias_cut[:, 0], part[:, 0:1], None, ALU.mult))
            done(dve.scalar_tensor_tensor(bias_sum[:, 1], bias_cut[:, 1], part[:, 1:2], bias_sum[:, 0], ALU.mult, ALU.add))
            dve.scalar_tensor_tensor(bias_parts[:], bias_cut[:, 2], part[:, 2:3], bias_sum[:, 1], ALU.mult, ALU.add)
            dve.memset(one_rows[:], 1.0)
            dve.memset(B.shift[:], 0.0)
            dve.tensor_copy(A.shift[32:64, :], future[0:32, :])
            dve.tensor_copy(A.shift[64:96, :], future[32:64, :])
            dve.tensor_copy(w_in[:], w_int[:, 0:2])
            dve.tensor_copy(w_down[:], w_int[:, 2])
            dve.wait_ge(act_setup, 2)
            sin = sincos[:, 0].rearrange("p h i -> p (h i)")
            cos = sincos[:, 1].rearrange("p h i -> p (h i)")
            dve.tensor_scalar(rot_cos[:, :, 0], cos, 1 / W_SCALE, None, ALU.mult)
            dve.tensor_scalar(rot_cos[:, :, 1], cos, 1 / W_SCALE, None, ALU.mult)
            dve.tensor_scalar(rot_sin[:, :, 0], sin, -1 / W_SCALE, None, ALU.mult)
            done(dve.tensor_scalar(rot_sin[:, :, 1], sin, 1 / W_SCALE, None, ALU.mult))
            dve.sem_inc(setup_done, 1)

            def all_moments(t):
                dve.wait_ge(x_first_loaded, 16)
                for n, lag in enumerate((0, LAG_CROSS, LAG_FFN)):
                    q = later(t, -lag)
                    if not q.live:
                        q = pair_at(0, None, None)
                    elif n == 1:
                        dve.wait_ge(x_first_loaded, 16)
                        dve.wait_ge(A.x_updated, index(q, 1))
                    elif n == 2:
                        dve.wait_ge(x_first_loaded, 16)
                        dve.wait_ge(B.x_updated, index(q, 1))
                    elif q.first == 4 and q.counts is None:
                        dve.wait_ge(x_rest_loaded, 16)
                    dve.bn_stats(stats[:, n], x_of(q))
                dve.drain()
                for n in range(3):
                    last = dve.bn_aggr(moments[:, n], stats[:, n])
                last.then_inc(moments_ready, 1)

            @for_live_pairs
            def normalize(n, lag, p):
                dve.wait_ge(rstd_ready, index(later(p, lag), 1))
                if p.first >= 1:
                    dve.wait_ge(split_done[n], index(p))
                dve.tensor_scalar(normed[n][:], x_of(p), moments[:, n, 0:1], rstd[:, n:n + 1], ALU.subtract, ALU.mult).then_inc(normed_ready[n], 1)

            @for_live_pairs
            def rotate(p):
                dve.wait_ge(A.qkv_ready, index(p, 1))
                if p.first >= 1:
                    dve.wait_ge(A.rotated, index(p))
                qk = A.lin[:, 0:2 * D].rearrange("p (a n e) -> p a n e", a=2, e=2)
                n = D // 2
                full = [128, 2, n, 2]
                ra = rot_a[:].rearrange("p (a n) e -> p a n e", a=2)
                rb = rot_b[:].rearrange("p (a n) e -> p a n e", a=2)
                dve.tensor_tensor(ra.rearrange("p a n e -> p a (n e)"), A.lin[:, 0:2 * D].rearrange("p (a m) -> p a m", a=2),
                                  rot_cos[:].rearrange("p n e -> p (n e)").unsqueeze(1).broadcast_to([128, 2, D]), ALU.mult)
                for e in range(2):
                    last = dve.tensor_tensor(rb[:, :, :, e], qk[:, :, :, 1 - e],
                                             rot_sin[:, :, e].unsqueeze(1).broadcast_to([128, 2, n]), ALU.mult)
                last.then_inc(A.rotated_a, 1)

            @for_live_pairs
            def maximum(s, p):
                dve.wait_ge(s.scores_ready, index(p, 1))
                dve.tensor_reduce(s.neg_max[:], s.scores.rearrange("p b (h k) -> p (b h) k", k=SEQ), AX.X, ALU.max, negate=True).then_inc(s.max_ready, 1)

            @for_live_pairs
            def split_max(s, p):
                dve.wait_ge(s.max_ready, index(p, 1))
                halves = s.neg_max[:].bitcast(BF16).rearrange("p (h a) -> p h a", a=2)
                dve.tensor_tensor(halves[:, :, 0], s.neg_max[:], halves[:, :, 1], ALU.subtract).then_inc(s.max_split, 1)

            @for_live_pairs
            def invert(s, p):
                dve.wait_ge(s.mixed_ready, index(p, 1))
                dve.reciprocal(s.inv_sum[:], s.scores[:, 0, TOK:2 * TOK]).then_inc(s.inv_sum_ready, 1)

            @for_live_pairs
            def scale_mixed(s, p):
                dve.wait_ge(s.inv_sum_ready, index(p, 1))
                dve.tensor_tensor(s.mixedT[:], s.scores[:, 0, 0:TOK], s.inv_sum[:], ALU.mult).then_inc(s.mixedT_ready, 1)

            @for_live_pairs
            def add_residual(s, p):
                dve.wait_ge(s.projected, index(p, 1))
                dve.tensor_tensor(x_of(p), s.scores[:, 1, 0:D], x_of(p), ALU.add).then_inc(s.x_updated, 1)

            @for_live_pairs
            def ffn_gated(p):
                dve.wait_ge(F.tanh_ready, index(p, 1))
                dve.scalar_tensor_tensor(F.gated[:], F.tanh[:], 1.0, F.gate[:, 0:HIDDEN], ALU.add, ALU.mult).then_inc(F.gated_ready, 1)

            @for_live_pairs
            def ffn_hidden(p):
                dve.wait_ge(F.gated_ready, index(p, 1))
                if p.first >= 1:
                    dve.wait_ge(F.hidden_low, index(p))
                dve.scalar_tensor_tensor(F.hidden[:], F.up[:, 0:HIDDEN], 0.5 * DEQUANT * DEQUANT, F.gated[:], ALU.mult, ALU.mult).then_inc(F.hidden_ready, 1)

            @for_live_pairs
            def ffn_residual(p):
                dve.wait_ge(F.down_ready, index(p, 1))
                dve.scalar_tensor_tensor(x_of(p), F.gate[:, 0:D], DEQUANT, x_of(p), ALU.mult, ALU.add).then_inc(F.x_updated, 1)

            def step(at):
                all_moments(at(0))
                normalize(0, 0, at(0))
                normalize(1, LAG_CROSS, at(3))
                ffn_gated(at(8))
                ffn_hidden(at(8))
                normalize(2, LAG_FFN, at(7))
                invert(B, at(5))
                scale_mixed(B, at(5))
                invert(A, at(2))
                scale_mixed(A, at(2))
                add_residual(B, at(5))
                rotate(at(0))
                add_residual(A, at(2))
                ffn_residual(at(8))
                maximum(B, at(4))
                split_max(B, at(4))
                maximum(A, at(1))
                split_max(A, at(1))

            run(dve, step)

        @block.tensor
        def _(pe):
            pe.wait_ge(const_loaded, 16 * N_CONST)
            pe.wait_ge(setup_done, 1)
            pe.wait_ge(slots_cleared, 1)

            def mm(o, lhsT, rhs, start):
                return pe.matmul(o, lhsT, rhs, start=start, stop=True, skip_group_check=True)

            def turn_parts(bank, n, parts):
                turned = bank.bitcast(F16)
                for half in range(2):
                    at = (2 * n + half) * TOK
                    last = pe.transpose(turned[:, at:at + TOK], parts[:, half], ident16[:])
                return last

            @for_live_pairs
            def turn_self(p):
                pe.wait_ge(split_done[0], index(p, 1))
                if p.first >= 1:
                    pe.wait_ge(A.stacked_ready, index(p))
                turn_parts(A.lin, 0, split[0]).then_inc(A.inputs_turned, 1)

            @for_live_pairs
            def turn_cross(p):
                pe.wait_ge(split_done[1], index(p, 1))
                pe.wait_ge(split_done[3], index(p, 1))
                if p.first >= 1:
                    pe.wait_ge(B.stacked_ready, index(p))
                turn_parts(B.lin, 0, split[1])
                turn_parts(B.lin, 1, split[3]).then_inc(B.inputs_turned, 1)

            @for_live_pairs
            def turn_ffn(p):
                pe.wait_ge(split_done[2], index(p, 1))
                if p.first >= 1:
                    pe.wait_ge(F.x_updated, index(p))
                turn_parts(F.gate, 0, split[2]).then_inc(F.input_turned, 1)

            @for_live_pairs
            def self_qkv(p):
                pe.wait_ge(A.inputsT_ready, index(p, 1))
                mm(A.lin[:, 0:3 * D], A.inputsT[:, 0, 0], w_self16[:, 0], True)
                mm(A.lin[:, 0:3 * D], A.inputsT[:, 0, 0], w_self16[:, 1], False)
                mm(A.lin[:, 0:3 * D], A.inputsT[:, 0, 1], w_self16[:, 0], False).then_inc(A.qkv_ready, 1)

            @for_live_pairs
            def cross_qkv(p):
                pe.wait_ge(B.inputsT_ready, index(p, 1))
                mm(B.lin[:, 0:3 * D], one_rows[:], bias_parts[:, 0:3 * D], True)
                for part_in, part_w in ((0, 0), (0, 1), (1, 0)):
                    mm(B.lin[:, 0:D], B.inputsT[:, 0, part_in], w_cross16[:, part_w, 0:D], False)
                    last = mm(B.lin[:, D:3 * D], B.inputsT[:, 1, part_in], w_cross16[:, part_w, D:3 * D], False)
                last.then_inc(B.qkv_ready, 1)

            @for_live_pairs
            def turn_slots(s, p):
                pe.wait_ge(s.low_ready, index(p, 1))
                pe.wait_ge(s.values_ready, index(p, 1))
                turned = s.lin.bitcast(F16)
                for n in range(2):
                    for g in range(GROUPS):
                        at = (n * GROUPS + g) * TOK
                        last = pe.transpose(turned[:, at:at + TOK], s.slots[:, n, 4 * g:4 * g + 4, :].rearrange("p h s -> p (h s)"), ident16[:])
                last.then_inc(s.slots_turned, 1)

            @for_live_pairs
            def mask_scores(p):
                if p.first >= 1:
                    pe.wait_ge(A.x_updated, index(p))
                for n in range(2):
                    mm(A.scores[:, n, :], future[:], key_is[:], True)

            @for_live_pairs
            def scores(s, p):
                pe.wait_ge(s.diag_ready[p.u], p.half * 64 + 64)
                if not s.causal:
                    if p.first >= 1:
                        pe.wait_ge(s.x_updated, index(p))
                for g in range(GROUPS):
                    for b in range(2):
                        cols = slice(g * TOK + b * SEQ, g * TOK + (b + 1) * SEQ)
                        last = mm(s.scores[SEQ * b:SEQ * (b + 1), g // 2, 256 * (g % 2):256 * (g % 2 + 1)],
                                  s.stacked[:, p.u, 0, cols], s.key_diag[:, p.u, 2 * g + b].rearrange("p h k -> p (h k)"), not s.causal and g % 2 == 0)
                last.then_inc(s.scores_ready, 1)

            def scoresT_bank(s, p, n):
                for m in range(4):
                    hp = 4 * n + m
                    for b in range(2):
                        cols = slice(hp // 2 * TOK + b * SEQ, hp // 2 * TOK + (b + 1) * SEQ)
                        mm(s.scores[:, n, m * TOK + b * SEQ:m * TOK + (b + 1) * SEQ],
                           s.key_diag[:, p.u, hp // 2 * 2 + b, 2 * (hp % 2):2 * (hp % 2) + 2].rearrange("p h k -> p (h k)"), s.stacked[:, p.u, 0, cols],
                           m == 0 and b == 0)

            @for_live_pairs
            def turn_max(s, p):
                pe.wait_ge(s.max_split, index(p, 1))
                pe.transpose(s.scores[0:2 * HEADS, 1, 0:TOK // 2].bitcast(BF16), s.neg_max[:].bitcast(BF16), identb[:]).then_inc(s.max_turned, 1)

            @for_live_pairs
            def scoresT_first(s, p):
                pe.wait_ge(s.max_ready, index(p, 1))
                scoresT_bank(s, p, 0)

            @for_live_pairs
            def scoresT_rest(s, p):
                pe.wait_ge(s.shift_ready, index(p, 1))
                scoresT_bank(s, p, 1)
                for hp in range(HPAIRS):
                    last = mm(s.scores[:, hp // 4, (hp % 4) * TOK:(hp % 4 + 1) * TOK], shift_pick[:, hp, :], s.shift[:], False)
                last.then_inc(s.scoresT_ready, 1)

            @for_live_pairs
            def sum_weights(s, p):
                pe.wait_ge(s.probs_ready, index(p, 1))
                for i in range(2):
                    for j in range(4):
                        hp = 2 * j + i
                        mm(s.scores[32 * j:32 * j + 32, 0, TOK:2 * TOK], ones[:, i, :], s.probs[:, hp * TOK:(hp + 1) * TOK], i == 0)

            @for_live_pairs
            def mix(s, p):
                for i in range(2):
                    for b in range(2):
                        for j in range(4):
                            hp = 2 * j + i
                            v = s.values[:, p.u, 4 * b + j, 2 * i:2 * i + 2, :].rearrange("p c d -> p (c d)")
                            last = mm(s.scores[32 * j:32 * j + 32, 0, SEQ * b:SEQ * (b + 1)], v,
                                      s.probs[:, hp * TOK + b * SEQ:hp * TOK + (b + 1) * SEQ], False)
                last.then_inc(s.mixed_ready, 1)

            @for_live_pairs
            def project(s, w, p):
                pe.wait_ge(s.mixedT_ready, index(p, 1))
                if not s.causal:
                    mm(s.scores[:, 1, 0:D], one_rows[:], bias_parts[:, 4 * D:5 * D], True)
                mm(s.scores[:, 1, 0:D], s.mixedT[:], w[:], s.causal).then_inc(s.projected, 1)

            @for_live_pairs
            def gate_up(p):
                pe.wait_ge(F.inputT_ready, index(p, 1))
                if p.first >= 1:
                    pe.wait_ge(F.hidden_ready, index(p))
                for n, bank in ((0, F.gate), (1, F.up)):
                    for c in range(CHUNKS):
                        for half in range(2):
                            last = mm(bank[:, c * TOK:(c + 1) * TOK], w_in[:, n, c * 128:(c + 1) * 128], F.inputT[:, half], half == 0)
                last.then_inc(F.gate_up_ready, 1)

            @for_live_pairs
            def down(p):
                pe.wait_ge(F.hidden_low, index(p, 1))
                for c in range(CHUNKS):
                    for half in range(2):
                        last = mm(F.gate[:, 0:D], F.hidden16[:, half, c * TOK:(c + 1) * TOK], w_down[:, c * D:(c + 1) * D], c == 0 and half == 0)
                last.then_inc(F.down_ready, 1)

            def step(at):
                sum_weights(B, at(5))
                mix(B, at(5))
                sum_weights(A, at(2))
                turn_cross(at(3))
                mix(A, at(2))
                turn_self(at(0))
                cross_qkv(at(3))
                project(B, w_cross_out, at(5))
                self_qkv(at(0))
                down(at(8))
                project(A, w_self_out, at(2))
                scores(B, at(4))
                mask_scores(at(1))
                turn_ffn(at(7))
                turn_slots(B, at(3))
                scores(A, at(1))
                turn_max(B, at(4))
                scoresT_first(B, at(4))
                gate_up(at(7))
                scoresT_rest(B, at(4))
                turn_max(A, at(1))
                turn_slots(A, at(0))
                scoresT_first(A, at(1))
                scoresT_rest(A, at(1))

            run(pe, step)


def kernel(**inputs):
    import numpy as _np
    import concourse.bacc as _bacc
    from concourse import mybir as _mybir
    from concourse.bass_utils import run_bass_kernel_spmd as _run

    def flat(name):
        return _np.ascontiguousarray(_np.asarray(inputs[name]).reshape(-1, D))

    def turned(name):
        return _np.ascontiguousarray(_np.asarray(inputs[name]).T)

    def row(name):
        return _np.ascontiguousarray(_np.asarray(inputs[name]))

    arrays = {
        "x": flat("x"), "ctx": flat("ctx_1024"),
        "w_qkvT": turned("L0_attn_Wqkv"), "w_self_outT": turned("L0_attn_Wo"),
        "log_xi": row("L0_attn_log_xi"), "pi_gate": row("L0_attn_pi_gate_logit"), "e_gate": row("L0_attn_e_gate_logit"),
        "w_qT": turned("L0_xattn_W_q"), "w_kT": turned("L0_xattn_W_k"), "w_vT": turned("L0_xattn_W_v"),
        "w_cross_outT": turned("L0_xattn_W_o"),
        "b_q": row("L0_xattn_b_q"), "b_k": row("L0_xattn_b_k"), "b_v": row("L0_xattn_b_v"), "b_o": row("L0_xattn_b_o"),
        "w_gateT": turned("L0_ffn_w_gate"), "w_upT": turned("L0_ffn_w_up"), "w_downT": turned("L0_ffn_w_down"),
        **constants(),
    }
    nc = _bacc.Bacc("TRN2", target_bir_lowering=False, num_devices=1)
    aps = {n: nc.dram_tensor(f"in_{n}", v.shape, _mybir.dt.from_np(v.dtype), kind="ExternalInput").ap() for n, v in arrays.items()}
    out = nc.dram_tensor("out_x", (BATCH * SEQ, D), F32, kind="ExternalOutput").ap()
    aps["out_flat"] = out
    build(nc, aps, out)
    r = _run(nc, [{f"in_{n}": v for n, v in arrays.items()}], core_ids=[0])
    return _np.asarray(r.results[0]["out_x"]).reshape(BATCH, SEQ, D)
```

```python
from contextlib import ExitStack

import numpy as np
import concourse.bass as bass
from concourse import mybir

F32 = mybir.dt.float32
F16 = mybir.dt.float16
BF16 = mybir.dt.bfloat16
I32 = mybir.dt.int32
ALU = mybir.AluOpType
ACT = mybir.ActivationFunctionType
AX = mybir.AxisListType

BATCH, SEQ, D = 128, 64, 128
HEADS, DH = 16, 8
HIDDEN = 384
CHUNKS = HIDDEN // 128
TOK = 2 * SEQ
PAIRS = BATCH * SEQ // TOK
SLOT = 32
GROUPS = HEADS * SLOT // 128
HPAIRS = HEADS // 2
EPS = 1e-5
SCORE_SCALE = float(DH) ** -0.5
DEQUANT = 1.0 / 127.0
W_SCALE = 16.0
MASKED = -1e30
MAX_DECAY = 336.0
SHIFT_ROWS = 2 * HEADS + SEQ
LAG_CROSS = 3
LAG_FFN = 7
LAST_LAG = 8
UNROLL = 6
PEELED = LAST_LAG + 2
PEELED += (PAIRS - PEELED) % UNROLL
assert PEELED % 2 == 0 and UNROLL % 2 == 0
TWO_PI = 2 * np.pi
TWO_PI_HIGH = 6.28125
ROUND = 1.5 * 2.0 ** 23
X_FIRST, X_SECOND = 4, PEELED - 1


class Indices:
    def __init__(self, eng, i):
        self.eng, self.i, self.known = eng, i, {}

    def __getitem__(self, n):
        if n not in self.known:
            register = self.eng.alloc_register(f"index_{n}")
            self.eng.reg_mov(register, self.i + n)
            self.known[n] = self.eng.snap(register, min_val=n, max_val=PAIRS - PEELED - UNROLL + n)
        return self.known[n]


class Record:
    pass


def constants():
    tok = np.arange(TOK)
    k = tok % SEQ
    future = np.where(np.arange(SEQ)[:, None] > k[None, :], MASKED, 0.0)
    shift_pick = np.zeros((SHIFT_ROWS, HPAIRS, 2, SEQ), np.float32)
    for h in range(HEADS):
        shift_pick[2 * h:2 * h + 2, h // 2, h % 2] = 1
    for j in range(SEQ):
        shift_pick[2 * HEADS + j, :, :, j] = 1
    ones = np.zeros((2, SEQ, 2, 4, DH), np.float32)
    for h2 in range(2):
        for i in range(2):
            ones[h2, :, i, 2 * i + h2] = 1
    freq = np.float32(np.pi) ** (np.float32(1) - np.arange(0, DH, 2, dtype=np.float32) / np.float32(DH))
    def packed(dt, *parts):
        out = np.zeros((128, sum(p.shape[1] for p in parts)), mybir.dt.np(dt))
        at = 0
        for p in parts:
            out[:p.shape[0], at:at + p.shape[1]] = p
            at += p.shape[1]
        return out

    return {
        "c_float": packed(F32, k[:, None] * freq[None, :], k[:, None], ones.reshape(128, 2 * 4 * DH)),
        "c_half": np.eye(128, dtype=np.float16),
        "c_bfloat": packed(BF16, np.eye(128), future, np.tile(np.eye(SEQ), (1, 8)), shift_pick.reshape(SHIFT_ROWS, HPAIRS * 128)),
    }


def build(nc, a, out):
    x_d = a["x"].rearrange("(p t) d -> t p d", t=TOK)
    out_d = out.rearrange("(p t) d -> t p d", t=TOK)

    with ExitStack() as ctx:
        def sb(name, shape, dt=F32):
            return ctx.enter_context(nc.sbuf_tensor(name, shape, dt))

        def sem(name):
            return ctx.enter_context(nc.semaphore(name))

        psum = ctx.enter_context(nc.psum_tensor("psum", [128, 8, 512], F32))

        c_float = sb("c_float", [128, DH // 2 + 1 + 2 * 4 * DH])
        angle, kpos = c_float[:, 0:DH // 2], c_float[:, DH // 2:DH // 2 + 1]
        ones = c_float[:, DH // 2 + 1:].rearrange("p (i m) -> p i m", i=2)
        ident16 = sb("ident16", [128, 128], F16)
        c_bfloat = sb("c_bfloat", [128, 128 + TOK + 8 * SEQ + HPAIRS * 128], BF16)
        identb, future, key_is = c_bfloat[:, 0:128], c_bfloat[0:SEQ, 128:128 + TOK], c_bfloat[0:SEQ, 128 + TOK:128 + TOK + 8 * SEQ]
        shift_pick = c_bfloat[0:SHIFT_ROWS, 128 + TOK + 8 * SEQ:].rearrange("p (h n) -> p h n", h=HPAIRS)
        w_both = sb("w_both", [128, 8 * D])
        w_self, w_self_out = w_both[:, 0:3 * D], w_both[:, 3 * D:4 * D]
        w_cross, w_cross_out = w_both[:, 4 * D:7 * D], w_both[:, 7 * D:8 * D]
        w_self16 = sb("w_self16", [128, 2, 3 * D], F16)
        w_cross16 = sb("w_cross16", [128, 2, 3 * D], F16)
        w_int = sb("w_int", [128, 3, HIDDEN], I32)
        w_in = sb("w_in", [128, 2, HIDDEN], F16)
        w_down = sb("w_down", [128, HIDDEN], F16)
        gates = sb("gates", [128, 3, HEADS])
        biases = sb("biases", [128, 3, D])
        value_bias = sb("value_bias", [128, 1])
        value_bias_row = sb("value_bias_row", [128, TOK])
        qk_bias = sb("qk_bias", [128, 2 * D])
        out_bias = sb("out_bias", [128, D])
        minus_half = sb("minus_half", [128, 1])
        eps = sb("eps", [128, 1])
        one = sb("one", [128, 1])

        gate_tanh = sb("gate_tanh", [128, 3, HEADS])
        gate = sb("gate", [128, 3, HEADS])
        inv_xi = sb("inv_xi", [128, HEADS])
        theta = sb("theta", [128, HEADS, DH // 2])
        turns = sb("turns", [128, 2, HEADS, DH // 2])
        reduced = sb("reduced", [128, 2, HEADS, DH // 2])
        sincos = sb("sincos", [128, 2, HEADS, DH // 2])
        rot_cos = sb("rot_cos", [128, HEADS * DH // 2, 2])
        rot_sin = sb("rot_sin", [128, HEADS * DH // 2, 2])
        decay = sb("decay", [128, HEADS])
        decay_rest = sb("decay_rest", [128, 2, HEADS])

        x_all = sb("x_all", [128, PAIRS * D])
        context = sb("context", [128, 2, D])

        first_loaded = sem("first_loaded")
        self_loaded = sem("self_loaded")
        late_loaded = sem("late_loaded")
        x_first_loaded = sem("x_first_loaded")
        x_second_loaded = sem("x_second_loaded")
        x_rest_loaded = sem("x_rest_loaded")
        self_slots_cleared = sem("self_slots_cleared")
        self_cleared = sem("self_cleared")
        cross_cleared = sem("cross_cleared")
        late_setup_done = sem("late_setup_done")
        dve_setup = sem("dve_setup")
        act_setup = sem("act_setup")
        angles_ready = sem("angles_ready")
        setup_done = sem("setup_done")
        context_loaded = [sem(f"context_loaded{u}") for u in range(2)]
        stored = sem("stored")

        stats = sb("stats", [128, 3, 6])
        moments = sb("moments", [128, 3, 2])
        var_eps = sb("var_eps", [128, 3])
        rstd = sb("rstd", [128, 3])
        moments_ready = sem("moments_ready")
        var_ready = sem("var_ready")
        rstd_ready = sem("rstd_ready")
        split_high = [sem(f"{n}_input_high") for n in ("self", "cross", "ffn", "context")]
        split_done = [sem(f"{n}_input_split") for n in ("self", "cross", "ffn", "context")]
        normed_ready = [sem(f"{n}_normed_ready") for n in ("self", "cross", "ffn")]
        normed = [sb(f"{n}_normed", [128, D]) for n in ("self", "cross", "ffn")]
        split = [sb(f"{n}_split", [128, 2, D], F16) for n in ("self", "cross", "ffn", "context")]

        def attention_state(n, bank, score_bank):
            s = Record()
            s.causal = n == "self"
            s.cleared = self_cleared if s.causal else cross_cleared
            s.lin, s.scores = psum[:, bank, :], psum[:, score_bank:score_bank + 2, :]
            s.inputsT = sb(f"{n}_inputsT", [128, 2, 2, TOK], F16)
            s.slots = sb(f"{n}_slots", [128, 2, HEADS, SLOT], F16)
            s.stacked = sb(f"{n}_stacked", [128, 2, 2, GROUPS * TOK], F16)
            s.key_diag = sb(f"{n}_key_diag", [128, 2, 2 * GROUPS, 4, SEQ], F16)
            s.values = sb(f"{n}_values", [128, 2, 8, 4, 2 * DH])
            s.neg_max = sb(f"{n}_neg_max", [128, HEADS])
            s.shift = sb(f"{n}_shift", [SHIFT_ROWS, TOK], BF16)
            s.probs = sb(f"{n}_probs", [128, HPAIRS * TOK])
            s.inv_sum = sb(f"{n}_inv_sum", [128, TOK])
            s.mixedT = sb(f"{n}_mixedT", [128, TOK])
            s.inputs_turned = sem(f"{n}_inputs_turned")
            s.inputsT_ready = sem(f"{n}_inputsT_ready")
            s.qkv_ready = sem(f"{n}_qkv_ready")
            s.rotated_a = sem(f"{n}_rotated_a")
            s.rotated = sem(f"{n}_rotated")
            s.high_ready = sem(f"{n}_high_ready")
            s.values_ready = sem(f"{n}_values_ready")
            s.low_ready = sem(f"{n}_low_ready")
            s.slots_turned = sem(f"{n}_slots_turned")
            s.stacked_ready = sem(f"{n}_stacked_ready")
            s.scores_ready = sem(f"{n}_scores_ready")
            s.max_ready = sem(f"{n}_max_ready")
            s.max_split = sem(f"{n}_max_split")
            s.max_turned = sem(f"{n}_max_turned")
            s.shift_ready = sem(f"{n}_shift_ready")
            s.scoresT_ready = sem(f"{n}_scoresT_ready")
            s.probs_ready = sem(f"{n}_probs_ready")
            s.mixed_ready = sem(f"{n}_mixed_ready")
            s.inv_sum_ready = sem(f"{n}_inv_sum_ready")
            s.mixedT_ready = sem(f"{n}_mixedT_ready")
            s.projected = sem(f"{n}_projected")
            s.x_updated = sem(f"{n}_x_updated")
            s.diag_ready = [sem(f"{n}_diag_ready{u}") for u in range(2)]
            return s

        A = attention_state("self", 4, 0)
        B = attention_state("cross", 5, 2)
        rot_a = sb("rot_a", [128, 2 * D // 2, 2])
        rot_b = sb("rot_b", [128, 2 * D // 2, 2])
        rot = sb("rot", [128, 2, HEADS, DH])
        cross_qk = sb("cross_qk", [128, 2, HEADS, DH])
        cross_qk_ready = sem("cross_qk_ready")
        x_biased = sem("x_biased")
        value_bias_ready = sem("value_bias_ready")
        out_bias_projected = sem("out_bias_projected")
        out_bias_ready = sem("out_bias_ready")
        F = Record()
        F.gate, F.up = psum[:, 6, :], psum[:, 7, :]
        F.inputT = sb("ffn_inputT", [128, 2, TOK], F16)
        F.tanh = sb("ffn_tanh", [128, HIDDEN])
        F.gated = sb("ffn_gated", [128, HIDDEN])
        F.hidden = sb("ffn_hidden", [128, HIDDEN])
        F.hidden16 = sb("ffn_hidden16", [128, 2, HIDDEN], F16)
        F.input_turned = sem("ffn_input_turned")
        F.inputT_ready = sem("ffn_inputT_ready")
        F.gate_up_ready = sem("ffn_gate_up_ready")
        F.tanh_ready = sem("ffn_tanh_ready")
        F.gated_ready = sem("ffn_gated_ready")
        F.hidden_ready = sem("ffn_hidden_ready")
        F.hidden_high = sem("ffn_hidden_high")
        F.hidden_low = sem("ffn_hidden_low")
        F.down_ready = sem("ffn_down_ready")
        F.x_updated = sem("ffn_x_updated")

        def pair_at(n0, i, counts):
            p = Record()
            p.first = n0
            p.u = n0 % 2
            p.live = i is not None or 0 <= n0 < PAIRS
            p.counts = counts
            p.loop = i
            return p

        def index(p, ahead=0):
            return p.first + ahead if p.counts is None else p.counts[p.first + ahead]

        def half_count(p, each, ahead=0):
            count = (p.first // 2 + 1 + ahead) * each
            return count if p.loop is None else p.loop * (each // 2) + count

        def later(p, n):
            return pair_at(p.first + n, p.loop, p.counts)

        def for_live_pairs(work):
            def guarded(*args):
                if args[-1].live:
                    work(*args)
            return guarded

        def run(eng, step, ahead):
            for t in range(PEELED):
                if t in ahead:
                    ahead[t]()
                step(lambda lag: pair_at(t - lag, None, None))
            with eng.Fori(0, PAIRS - PEELED, UNROLL) as i:
                indices = Indices(eng, i)
                for t in range(PEELED, PEELED + UNROLL):
                    step(lambda lag: pair_at(t - lag, i, indices))
            for t in range(PAIRS, PAIRS + LAST_LAG):
                step(lambda lag: pair_at(t - lag, None, None))

        def x_of(p):
            return x_all[:, bass.ds(index(p) * D, D)]

        def x_chunk(first, last):
            return x_all[:, first * D:last * D].rearrange("t (p d) -> t p d", d=D)

        block = ctx.enter_context(nc.Block())

        @block.sync
        def _(sp):
            sp.dma_start(c_float[:], a["c_float"]).then_inc(first_loaded, 16)
            sp.dma_start(x_chunk(0, X_FIRST), x_d[:, 0:X_FIRST, :]).then_inc(x_first_loaded, 16)
            sp.dma_start(w_both[:, 0:4 * D], a["w_both"][:, 0:4 * D]).then_inc(self_loaded, 16)
            sp.dma_start(ident16[:], a["c_half"]).then_inc(self_loaded, 16)
            sp.dma_start(x_chunk(X_FIRST, X_SECOND), x_d[:, X_FIRST:X_SECOND, :]).then_inc(x_second_loaded, 16)

            @for_live_pairs
            def load_context(p):
                if p.first >= 2:
                    sp.wait_ge(split_done[3], index(p, -1))
                sp.dma_start(context[:, p.u, :], a["ctx"][bass.ds(index(p) * TOK, TOK), :]).then_inc(context_loaded[p.u], 16)

            @for_live_pairs
            def spread_keys(s, p):
                if p.first < 2:
                    sp.wait_ge(s.cleared, 1)
                if p.first >= 2:
                    sp.wait_ge(s.scoresT_ready, index(p, -1))
                sp.wait_ge(s.stacked_ready, index(p, 1))
                for h in range(4):
                    rows = slice(SLOT * h, SLOT * (h + 1))
                    sp.dma_start(s.key_diag[rows, p.u, :, h, :], s.stacked[rows, p.u, 1, :].rearrange("p (n k) -> p n k", k=SEQ)).then_inc(s.diag_ready[p.u], 16)

            @for_live_pairs
            def store(p):
                rows = a["out_flat"][bass.ds(index(p) * TOK, TOK), :]
                sp.wait_ge(F.x_updated, index(p, 1))
                sp.dma_start(rows, x_of(p)).then_inc(stored, 16)

            def load_rest(n):
                first, last = (X_SECOND + (PAIRS - X_SECOND) * m // 4 for m in (n, n + 1))
                sp.dma_start(x_chunk(first, last), x_d[:, first:last, :]).then_inc(x_rest_loaded, 16)

            def step(at):
                load_context(at(2))
                spread_keys(A, at(1))
                spread_keys(B, at(3))
                store(at(8))

            run(sp, step, {n + 1: (lambda n=n: load_rest(n)) for n in range(4)})
            sp.wait_ge(stored, 16 * PAIRS)

        @block.gpsimd
        def _(pool):
            pool.memset(minus_half[:], -0.5)
            pool.memset(eps[:], EPS)
            pool.memset(one[:], 1.0)
            pool.memset(A.slots[:], 0.0).then_inc(self_slots_cleared, 1)
            pool.memset(A.key_diag[:], 0.0)
            pool.memset(A.values[:], 0.0).then_inc(self_cleared, 1)
            pool.wait_ge(self_cleared, 1)

            def clear_cross():
                pool.memset(B.slots[:], 0.0)
                pool.memset(B.shift[:], 0.0)
                pool.memset(B.values[:], 0.0)
                pool.memset(B.key_diag[:], 0.0).then_inc(cross_cleared, 1)
                pool.wait_ge(cross_cleared, 1)

            def inverse_deviation(t):
                pool.wait_ge(moments_ready, index(t, 1))
                pool.tensor_tensor(var_eps[:], moments[:, :, 1], eps[:].broadcast_to([128, 3]), ALU.add).then_inc(var_ready, 1)
                pool.wait_ge(var_ready, index(t, 1))
                pool.tensor_tensor(rstd[:], var_eps[:], minus_half[:].broadcast_to([128, 3]), ALU.pow).then_inc(rstd_ready, 1)

            @for_live_pairs
            def add_rotation(p):
                pool.wait_ge(A.rotated_a, index(p, 1))
                if p.first >= 1:
                    pool.wait_ge(A.high_ready, index(p))
                if p.first >= 1:
                    pool.wait_ge(A.low_ready, index(p))
                pool.tensor_tensor(rot[:].rearrange("p a h d -> p (a h d)"), rot_a[:].rearrange("p a b -> p (a b)"),
                                   rot_b[:].rearrange("p a b -> p (a b)"), ALU.add).then_inc(A.rotated, 1)

            @for_live_pairs
            def split_low(p):
                pool.wait_ge(A.high_ready, index(p, 1))
                pool.tensor_tensor(A.slots[:, 0, :, 16:24], rot[:, 0], A.slots[:, 0, :, 0:8], ALU.subtract)
                pool.tensor_tensor(A.slots[:, 1, :, 8:16], rot[:, 1], A.slots[:, 1, :, 0:8], ALU.subtract).then_inc(A.low_ready, 1)

            def split_input(n, source, turned, p):
                if p.first >= 1:
                    pool.wait_ge(turned, index(p))
                pool.tensor_tensor(split[n][:, 0], source, one[:].broadcast_to([128, D]), ALU.mult).then_inc(split_high[n], 1)
                pool.wait_ge(split_high[n], index(p, 1))
                pool.tensor_tensor(split[n][:, 1], source, split[n][:, 0], ALU.subtract).then_inc(split_done[n], 1)

            @for_live_pairs
            def split_self(p):
                pool.wait_ge(normed_ready[0], index(p, 1))
                split_input(0, normed[0][:], A.inputs_turned, p)

            @for_live_pairs
            def split_cross(p):
                pool.wait_ge(normed_ready[1], index(p, 1))
                split_input(1, normed[1][:], B.inputs_turned, p)

            @for_live_pairs
            def split_ffn(p):
                pool.wait_ge(normed_ready[2], index(p, 1))
                split_input(2, normed[2][:], F.input_turned, p)

            @for_live_pairs
            def split_context(p):
                pool.wait_ge(context_loaded[p.u], half_count(p, 16))
                split_input(3, context[:, p.u, :], B.inputs_turned, p)

            @for_live_pairs
            def add_out_bias(p):
                pool.wait_ge(normed_ready[1], index(p, 1))
                pool.tensor_tensor(x_of(p), x_of(p), out_bias[:], ALU.add).then_inc(x_biased, 1)

            @for_live_pairs
            def cross_low(p):
                pool.wait_ge(B.high_ready, index(p, 1))
                pool.tensor_tensor(B.slots[:, 0, :, 16:24], cross_qk[:, 0], B.slots[:, 0, :, 0:8], ALU.subtract)
                pool.tensor_tensor(B.slots[:, 1, :, 8:16], cross_qk[:, 1], B.slots[:, 1, :, 0:8], ALU.subtract).then_inc(B.low_ready, 1)

            @for_live_pairs
            def hidden_low(p):
                pool.wait_ge(F.hidden_high, index(p, 1))
                pool.tensor_tensor(F.hidden16[:, 1], F.hidden[:], F.hidden16[:, 0], ALU.subtract).then_inc(F.hidden_low, 1)

            def step(at):
                split_context(at(3))
                add_rotation(at(1))
                inverse_deviation(at(0))
                split_low(at(1))
                split_cross(at(3))
                split_self(at(0))
                hidden_low(at(8))
                cross_low(at(3))
                split_ffn(at(7))
                add_out_bias(at(4))

            run(pool, step, {1: clear_cross, LAG_CROSS: lambda: pool.wait_ge(out_bias_ready, 1)})

        @block.scalar
        def _(act):
            act.dma_start(gates[:], a["gates"].partition_broadcast(128)).then_inc(first_loaded, 16)
            act.dma_start(c_bfloat[:], a["c_bfloat"]).then_inc(self_loaded, 16)
            act.dma_start(w_both[:, 4 * D:], a["w_both"][:, 4 * D:]).then_inc(late_loaded, 16)
            act.dma_start(w_int[:], a["w_int"]).then_inc(late_loaded, 16)
            act.dma_start(biases[:], a["biases"].partition_broadcast(128)).then_inc(late_loaded, 16)
            act.dma_start(value_bias[:], a["value_bias"]).then_inc(late_loaded, 16)
            act.wait_ge(first_loaded, 32)
            act.activation(inv_xi[:], gates[:, 0, :], ACT.Exp, scale=-1.0)
            act.activation(gate_tanh[:], gates[:], ACT.Tanh, scale=0.5).then_inc(act_setup, 1)
            act.wait_ge(angles_ready, 1)
            act.activation(sincos[:], reduced[:], ACT.Sin).then_inc(act_setup, 1)
            act.wait_ge(setup_done, 1)

            @for_live_pairs
            def turn_self_in(p):
                act.wait_ge(A.inputs_turned, index(p, 1))
                act.activation(A.inputsT[:, 0].rearrange("p a t -> p (a t)"), A.lin[:, 0:TOK].bitcast(F16), ACT.Copy).then_inc(A.inputsT_ready, 1)

            @for_live_pairs
            def turn_cross_in(p):
                act.wait_ge(B.inputs_turned, index(p, 1))
                act.activation(B.inputsT[:].rearrange("p n a t -> p (n a t)"), B.lin[:, 0:2 * TOK].bitcast(F16), ACT.Copy).then_inc(B.inputsT_ready, 1)

            @for_live_pairs
            def turn_ffn_in(p):
                act.wait_ge(F.input_turned, index(p, 1))
                act.activation(F.inputT[:].rearrange("p a t -> p (a t)"), F.gate[:, 0:TOK].bitcast(F16), ACT.Copy).then_inc(F.inputT_ready, 1)

            def high_parts(s, q, k):
                act.activation(s.slots[:, 0, :, 0:16].rearrange("p h (r d) -> p h r d", d=DH),
                               q.unsqueeze(2).broadcast_to([128, HEADS, 2, DH]), ACT.Copy)
                act.activation(s.slots[:, 1, :, 0:8], k, ACT.Copy)
                act.activation(s.slots[:, 1, :, 16:24], k, ACT.Copy).then_inc(s.high_ready, 1)

            @for_live_pairs
            def take_values(s, p):
                if p.first >= 2:
                    act.wait_ge(s.mixed_ready, index(p, -1))
                v = s.lin[:, 2 * D:3 * D].rearrange("p (j i t d) -> p j i t d", i=2, t=2, d=DH)
                for b in range(2):
                    for t in range(2):
                        last = act.activation(s.values[SEQ * t:SEQ * (t + 1), p.u, 4 * b:4 * b + 4, 0:4:3, t * DH:(t + 1) * DH],
                                              v[SEQ * b:SEQ * (b + 1), :, :, t, :], ACT.Copy, scale=1 / W_SCALE)
                last.then_inc(s.values_ready, 1)

            @for_live_pairs
            def self_values(p):
                act.wait_ge(A.rotated_a, index(p, 1))
                take_values(A, p)

            @for_live_pairs
            def self_high(p):
                act.wait_ge(A.rotated, index(p, 1))
                high_parts(A, rot[:, 0], rot[:, 1])

            @for_live_pairs
            def cross_values(p):
                act.wait_ge(cross_qk_ready, index(p, 1))
                take_values(B, p)

            @for_live_pairs
            def cross_high(p):
                act.wait_ge(cross_qk_ready, index(p, 1))
                high_parts(B, cross_qk[:, 0], cross_qk[:, 1])

            @for_live_pairs
            def take_shift(s, p):
                act.wait_ge(s.max_turned, index(p, 1))
                if p.first >= 1:
                    act.wait_ge(s.scoresT_ready, index(p))
                turned = s.scores[0:2 * HEADS, 1, 0:TOK // 2].bitcast(BF16)
                act.activation(s.shift[0:2 * HEADS, :], turned, ACT.Copy).then_inc(s.shift_ready, 1)

            @for_live_pairs
            def exponent(s, p):
                act.wait_ge(s.scoresT_ready, index(p, 1))
                act.activation(s.probs[:].rearrange("p (b n) -> p b n", b=2), s.scores, ACT.Exp,
                               scale=SCORE_SCALE if s.causal else SCORE_SCALE / W_SCALE ** 2).then_inc(s.probs_ready, 1)

            @for_live_pairs
            def ffn_tanh(p):
                act.wait_ge(F.gate_up_ready, index(p, 1))
                if p.first >= 1:
                    act.wait_ge(F.gated_ready, index(p))
                act.activation(F.tanh[:], F.gate[:, 0:HIDDEN], ACT.Tanh, scale=0.5 * DEQUANT).then_inc(F.tanh_ready, 1)

            @for_live_pairs
            def hidden_high(p):
                act.wait_ge(F.hidden_ready, index(p, 1))
                if p.first >= 1:
                    act.wait_ge(F.down_ready, index(p))
                act.activation(F.hidden16[:, 0], F.hidden[:], ACT.Copy).then_inc(F.hidden_high, 1)

            @for_live_pairs
            def take_stacked(s, p):
                act.wait_ge(s.slots_turned, index(p, 1))
                if p.first >= 2:
                    act.wait_ge(s.scoresT_ready, index(p, -1))
                    act.wait_ge(s.diag_ready[p.u], half_count(p, 64, -1))
                act.activation(s.stacked[:, p.u].rearrange("p a n -> p (a n)"), s.lin.bitcast(F16), ACT.Copy).then_inc(s.stacked_ready, 1)

            def step(at):
                turn_ffn_in(at(8))
                exponent(B, at(5))
                self_high(at(1))
                self_values(at(1))
                ffn_tanh(at(8))
                take_shift(A, at(2))
                take_stacked(A, at(1))
                turn_cross_in(at(3))
                exponent(A, at(2))
                hidden_high(at(8))
                cross_high(at(3))
                cross_values(at(3))
                turn_self_in(at(0))
                take_shift(B, at(4))
                take_stacked(B, at(3))

            run(act, step, {LAG_CROSS: lambda: act.wait_ge(cross_cleared, 1)})

        @block.vector
        def _(dve):
            count = [0]

            def done(ins):
                ins.then_inc(dve_setup, 1)
                count[0] += 1
                dve.wait_ge(dve_setup, count[0])

            dve.memset(stats[:], 1.0)
            dve.wait_ge(act_setup, 1)
            done(dve.tensor_scalar(gate[:], gate_tanh[:], 0.5, 0.5, ALU.mult, ALU.add))
            done(dve.tensor_tensor(theta[:], angle.unsqueeze(1).broadcast_to([128, HEADS, DH // 2]),
                                   gate[:, 1, :].unsqueeze(2).broadcast_to([128, HEADS, DH // 2]), ALU.mult))
            dve.tensor_scalar(turns[:, 0], theta[:], 1 / TWO_PI, ROUND, ALU.mult, ALU.add)
            done(dve.tensor_scalar(turns[:, 1], theta[:], 1 / TWO_PI, 0.25, ALU.mult, ALU.add))
            done(dve.tensor_scalar(turns[:, 1], turns[:, 1], ROUND, None, ALU.add))
            done(dve.tensor_scalar(turns[:], turns[:], -ROUND, None, ALU.add))
            for n in range(2):
                last = dve.scalar_tensor_tensor(reduced[:, n], turns[:, n], -TWO_PI_HIGH, theta[:], ALU.mult, ALU.add)
            done(last)
            flat = reduced[:].rearrange("p a h i -> p (a h i)")
            done(dve.scalar_tensor_tensor(flat, turns[:].rearrange("p a h i -> p (a h i)"), -(TWO_PI - TWO_PI_HIGH), flat, ALU.mult, ALU.add))
            done(dve.tensor_scalar(reduced[:, 1], reduced[:, 1], np.pi / 2, None, ALU.add))
            dve.tensor_scalar(reduced[:], reduced[:], 3.1415925, -3.1415925, ALU.min, ALU.max).then_inc(angles_ready, 1)
            done(dve.tensor_tensor(decay[:], inv_xi[:], gate[:, 2, :], ALU.mult))
            done(dve.tensor_scalar(decay[:], decay[:], MAX_DECAY, 1 / SCORE_SCALE, ALU.min, ALU.mult))
            done(dve.tensor_scalar(decay[:], decay[:], kpos, None, ALU.mult))
            dve.wait_ge(self_slots_cleared, 1)
            dve.memset(A.slots[:, 0, :, 24:27], 1.0)
            k1, k2, k3 = (A.slots[:, 1, :, n] for n in (24, 25, 26))
            done(dve.tensor_copy(k1, decay[:]))
            done(dve.tensor_tensor(decay_rest[:, 0], decay[:], k1, ALU.subtract))
            done(dve.tensor_copy(k2, decay_rest[:, 0]))
            done(dve.tensor_tensor(decay_rest[:, 1], decay_rest[:, 0], k2, ALU.subtract))
            dve.tensor_copy(k3, decay_rest[:, 1])
            def split_weights(w16, w):
                done(dve.tensor_scalar(w16[:, 0], w, W_SCALE, None, ALU.mult))
                dve.scalar_tensor_tensor(w16[:, 1], w, W_SCALE, w16[:, 0], ALU.mult, ALU.subtract)

            dve.wait_ge(self_loaded, 48)
            dve.tensor_copy(A.shift[32:64, :], future[0:32, :])
            dve.tensor_copy(A.shift[64:96, :], future[32:64, :])
            split_weights(w_self16, w_self)
            dve.wait_ge(act_setup, 2)
            sin = sincos[:, 0].rearrange("p h i -> p (h i)")
            cos = sincos[:, 1].rearrange("p h i -> p (h i)")
            dve.tensor_scalar(rot_cos[:, :, 0], cos, 1 / W_SCALE, None, ALU.mult)
            dve.tensor_scalar(rot_cos[:, :, 1], cos, 1 / W_SCALE, None, ALU.mult)
            dve.tensor_scalar(rot_sin[:, :, 0], sin, -1 / W_SCALE, None, ALU.mult)
            done(dve.tensor_scalar(rot_sin[:, :, 1], sin, 1 / W_SCALE, None, ALU.mult))
            dve.sem_inc(setup_done, 1)

            def late_setup():
                dve.wait_ge(late_loaded, 64)
                done(dve.tensor_copy(value_bias_row[:], value_bias[:].broadcast_to([128, TOK])))
                dve.sem_inc(value_bias_ready, 1)
                dve.tensor_scalar(qk_bias[:], biases[:, 0:2].rearrange("p a d -> p (a d)"), W_SCALE, None, ALU.mult)
                split_weights(w_cross16, w_cross)
                dve.tensor_copy(w_in[:], w_int[:, 0:2])
                done(dve.tensor_copy(w_down[:], w_int[:, 2]))
                dve.sem_inc(late_setup_done, 1)

            def add_up_out_bias():
                dve.wait_ge(out_bias_projected, 1)
                dve.tensor_tensor(out_bias[:], B.scores[:, 0, 0:D], biases[:, 2], ALU.add).then_inc(out_bias_ready, 1)

            def all_moments(t):
                dve.wait_ge(x_first_loaded, 16)
                for n, lag in enumerate((0, LAG_CROSS, LAG_FFN)):
                    q = later(t, -lag)
                    if not q.live:
                        continue
                    if n == 1:
                        dve.wait_ge(x_first_loaded, 16)
                        dve.wait_ge(A.x_updated, index(q, 1))
                    elif n == 2:
                        dve.wait_ge(x_first_loaded, 16)
                        dve.wait_ge(B.x_updated, index(q, 1))
                    elif q.first == X_FIRST and q.counts is None:
                        dve.wait_ge(x_second_loaded, 16)
                    elif q.first == PEELED - 1 and q.counts is None:
                        dve.wait_ge(x_rest_loaded, 64)
                    dve.bn_stats(stats[:, n], x_of(q))
                dve.drain()
                for n in range(3):
                    last = dve.bn_aggr(moments[:, n], stats[:, n])
                last.then_inc(moments_ready, 1)

            @for_live_pairs
            def normalize(n, lag, p):
                dve.wait_ge(rstd_ready, index(later(p, lag), 1))
                if p.first >= 1:
                    dve.wait_ge(split_done[n], index(p))
                dve.tensor_scalar(normed[n][:], x_of(p), moments[:, n, 0:1], rstd[:, n:n + 1], ALU.subtract, ALU.mult).then_inc(normed_ready[n], 1)

            @for_live_pairs
            def rotate(p):
                dve.wait_ge(A.qkv_ready, index(p, 1))
                if p.first >= 1:
                    dve.wait_ge(A.rotated, index(p))
                qk = A.lin[:, 0:2 * D].rearrange("p (a n e) -> p a n e", a=2, e=2)
                n = D // 2
                full = [128, 2, n, 2]
                ra = rot_a[:].rearrange("p (a n) e -> p a n e", a=2)
                rb = rot_b[:].rearrange("p (a n) e -> p a n e", a=2)
                dve.tensor_tensor(ra.rearrange("p a n e -> p a (n e)"), A.lin[:, 0:2 * D].rearrange("p (a m) -> p a m", a=2),
                                  rot_cos[:].rearrange("p n e -> p (n e)").unsqueeze(1).broadcast_to([128, 2, D]), ALU.mult)
                for e in range(2):
                    last = dve.tensor_tensor(rb[:, :, :, e], qk[:, :, :, 1 - e],
                                             rot_sin[:, :, e].unsqueeze(1).broadcast_to([128, 2, n]), ALU.mult)
                last.then_inc(A.rotated_a, 1)

            @for_live_pairs
            def add_qk_bias(p):
                dve.wait_ge(B.qkv_ready, index(p, 1))
                if p.first >= 1:
                    dve.wait_ge(B.low_ready, index(p))
                dve.tensor_tensor(cross_qk[:].rearrange("p a h d -> p (a h d)"), B.lin[:, 0:2 * D], qk_bias[:], ALU.add).then_inc(cross_qk_ready, 1)

            @for_live_pairs
            def maximum(s, p):
                dve.wait_ge(s.scores_ready, index(p, 1))
                dve.tensor_reduce(s.neg_max[:], s.scores.rearrange("p b (h k) -> p (b h) k", k=SEQ), AX.X, ALU.max, negate=True).then_inc(s.max_ready, 1)

            @for_live_pairs
            def split_max(s, p):
                dve.wait_ge(s.max_ready, index(p, 1))
                halves = s.neg_max[:].bitcast(BF16).rearrange("p (h a) -> p h a", a=2)
                dve.tensor_tensor(halves[:, :, 0], s.neg_max[:], halves[:, :, 1], ALU.subtract).then_inc(s.max_split, 1)

            @for_live_pairs
            def invert(s, p):
                dve.wait_ge(s.mixed_ready, index(p, 1))
                dve.reciprocal(s.inv_sum[:], s.scores[:, 0, TOK:2 * TOK]).then_inc(s.inv_sum_ready, 1)

            @for_live_pairs
            def scale_mixed(s, p):
                dve.wait_ge(s.inv_sum_ready, index(p, 1))
                dve.tensor_tensor(s.mixedT[:], s.scores[:, 0, 0:TOK], s.inv_sum[:], ALU.mult).then_inc(s.mixedT_ready, 1)

            @for_live_pairs
            def add_residual(s, p):
                dve.wait_ge(s.projected, index(p, 1))
                if not s.causal:
                    dve.wait_ge(x_biased, index(p, 1))
                dve.tensor_tensor(x_of(p), s.scores[:, 1, 0:D], x_of(p), ALU.add).then_inc(s.x_updated, 1)

            @for_live_pairs
            def ffn_gated(p):
                dve.wait_ge(F.tanh_ready, index(p, 1))
                dve.scalar_tensor_tensor(F.gated[:], F.tanh[:], 1.0, F.gate[:, 0:HIDDEN], ALU.add, ALU.mult).then_inc(F.gated_ready, 1)

            @for_live_pairs
            def ffn_hidden(p):
                dve.wait_ge(F.gated_ready, index(p, 1))
                if p.first >= 1:
                    dve.wait_ge(F.hidden_low, index(p))
                dve.scalar_tensor_tensor(F.hidden[:], F.up[:, 0:HIDDEN], 0.5 * DEQUANT * DEQUANT, F.gated[:], ALU.mult, ALU.mult).then_inc(F.hidden_ready, 1)

            @for_live_pairs
            def ffn_residual(p):
                dve.wait_ge(F.down_ready, index(p, 1))
                dve.scalar_tensor_tensor(x_of(p), F.gate[:, 0:D], DEQUANT, x_of(p), ALU.mult, ALU.add).then_inc(F.x_updated, 1)

            def step(at):
                all_moments(at(0))
                maximum(A, at(2))
                normalize(1, LAG_CROSS, at(3))
                split_max(A, at(2))
                ffn_gated(at(8))
                normalize(0, 0, at(0))
                invert(B, at(5))
                scale_mixed(B, at(5))
                ffn_hidden(at(8))
                add_residual(B, at(5))
                normalize(2, LAG_FFN, at(7))
                add_qk_bias(at(3))
                maximum(B, at(4))
                split_max(B, at(4))
                invert(A, at(2))
                ffn_residual(at(8))
                scale_mixed(A, at(2))
                rotate(at(0))
                add_residual(A, at(2))

            run(dve, step, {1: late_setup, LAG_CROSS: add_up_out_bias})

        @block.tensor
        def _(pe):
            pe.wait_ge(self_loaded, 48)
            pe.wait_ge(setup_done, 1)
            pe.wait_ge(self_cleared, 1)

            def mm(o, lhsT, rhs, start):
                return pe.matmul(o, lhsT, rhs, start=start, stop=True, skip_group_check=True)

            def turn_parts(bank, n, parts):
                turned = bank.bitcast(F16)
                for half in range(2):
                    at = (2 * n + half) * TOK
                    last = pe.transpose(turned[:, at:at + TOK], parts[:, half], ident16[:])
                return last

            @for_live_pairs
            def turn_self(p):
                pe.wait_ge(split_done[0], index(p, 1))
                if p.first >= 1:
                    pe.wait_ge(A.stacked_ready, index(p))
                turn_parts(A.lin, 0, split[0]).then_inc(A.inputs_turned, 1)

            @for_live_pairs
            def turn_cross(p):
                pe.wait_ge(split_done[1], index(p, 1))
                pe.wait_ge(split_done[3], index(p, 1))
                if p.first >= 1:
                    pe.wait_ge(B.stacked_ready, index(p))
                turn_parts(B.lin, 0, split[1])
                turn_parts(B.lin, 1, split[3]).then_inc(B.inputs_turned, 1)

            @for_live_pairs
            def turn_ffn(p):
                pe.wait_ge(split_done[2], index(p, 1))
                if p.first >= 1:
                    pe.wait_ge(F.x_updated, index(p))
                turn_parts(F.gate, 0, split[2]).then_inc(F.input_turned, 1)

            @for_live_pairs
            def self_qkv(p):
                pe.wait_ge(A.inputsT_ready, index(p, 1))
                mm(A.lin[:, 0:3 * D], A.inputsT[:, 0, 0], w_self16[:, 0], True)
                mm(A.lin[:, 0:3 * D], A.inputsT[:, 0, 0], w_self16[:, 1], False)
                mm(A.lin[:, 0:3 * D], A.inputsT[:, 0, 1], w_self16[:, 0], False).then_inc(A.qkv_ready, 1)

            @for_live_pairs
            def cross_qkv(p):
                pe.wait_ge(B.inputsT_ready, index(p, 1))
                for part_in, part_w in ((0, 0), (0, 1), (1, 0)):
                    mm(B.lin[:, 0:D], B.inputsT[:, 0, part_in], w_cross16[:, part_w, 0:D], part_in + part_w == 0)
                    last = mm(B.lin[:, D:3 * D], B.inputsT[:, 1, part_in], w_cross16[:, part_w, D:3 * D], False)
                last.then_inc(B.qkv_ready, 1)

            @for_live_pairs
            def turn_slots(s, p):
                pe.wait_ge(s.low_ready, index(p, 1))
                pe.wait_ge(s.values_ready, index(p, 1))
                turned = s.lin.bitcast(F16)
                for n in range(2):
                    for g in range(GROUPS):
                        at = (n * GROUPS + g) * TOK
                        last = pe.transpose(turned[:, at:at + TOK], s.slots[:, n, 4 * g:4 * g + 4, :].rearrange("p h s -> p (h s)"), ident16[:])
                last.then_inc(s.slots_turned, 1)

            @for_live_pairs
            def mask_scores(p):
                if p.first >= 1:
                    pe.wait_ge(A.x_updated, index(p))
                for n in range(2):
                    mm(A.scores[:, n, :], future, key_is, True)

            @for_live_pairs
            def scores(s, p):
                pe.wait_ge(s.diag_ready[p.u], half_count(p, 64))
                if not s.causal:
                    if p.first >= 1:
                        pe.wait_ge(s.x_updated, index(p))
                for g in range(GROUPS):
                    for b in range(2):
                        cols = slice(g * TOK + b * SEQ, g * TOK + (b + 1) * SEQ)
                        last = mm(s.scores[SEQ * b:SEQ * (b + 1), g // 2, 256 * (g % 2):256 * (g % 2 + 1)],
                                  s.stacked[:, p.u, 0, cols], s.key_diag[:, p.u, 2 * g + b].rearrange("p h k -> p (h k)"), not s.causal and g % 2 == 0)
                last.then_inc(s.scores_ready, 1)

            def scoresT_bank(s, p, n):
                for m in range(4):
                    hp = 4 * n + m
                    for b in range(2):
                        cols = slice(hp // 2 * TOK + b * SEQ, hp // 2 * TOK + (b + 1) * SEQ)
                        mm(s.scores[:, n, m * TOK + b * SEQ:m * TOK + (b + 1) * SEQ],
                           s.key_diag[:, p.u, hp // 2 * 2 + b, 2 * (hp % 2):2 * (hp % 2) + 2].rearrange("p h k -> p (h k)"), s.stacked[:, p.u, 0, cols],
                           m == 0 and b == 0)

            @for_live_pairs
            def turn_max(s, p):
                pe.wait_ge(s.max_split, index(p, 1))
                pe.transpose(s.scores[0:2 * HEADS, 1, 0:TOK // 2].bitcast(BF16), s.neg_max[:].bitcast(BF16), identb).then_inc(s.max_turned, 1)

            @for_live_pairs
            def scoresT_first(s, p):
                pe.wait_ge(s.max_ready, index(p, 1))
                scoresT_bank(s, p, 0)

            @for_live_pairs
            def scoresT_rest(s, p):
                pe.wait_ge(s.shift_ready, index(p, 1))
                scoresT_bank(s, p, 1)
                for hp in range(HPAIRS):
                    last = mm(s.scores[:, hp // 4, (hp % 4) * TOK:(hp % 4 + 1) * TOK], shift_pick[:, hp, :], s.shift[:], False)
                last.then_inc(s.scoresT_ready, 1)

            @for_live_pairs
            def sum_weights(s, p):
                pe.wait_ge(s.probs_ready, index(p, 1))
                for i in range(2):
                    for j in range(4):
                        hp = 2 * j + i
                        mm(s.scores[32 * j:32 * j + 32, 0, TOK:2 * TOK], ones[:, i, :], s.probs[:, hp * TOK:(hp + 1) * TOK], i == 0)

            @for_live_pairs
            def mix(s, p):
                for i in range(2):
                    for b in range(2):
                        for j in range(4):
                            hp = 2 * j + i
                            v = s.values[:, p.u, 4 * b + j, 2 * i:2 * i + 2, :].rearrange("p c d -> p (c d)")
                            last = mm(s.scores[32 * j:32 * j + 32, 0, SEQ * b:SEQ * (b + 1)], v,
                                      s.probs[:, hp * TOK + b * SEQ:hp * TOK + (b + 1) * SEQ], False)
                last.then_inc(s.mixed_ready, 1)

            @for_live_pairs
            def project(s, w, p):
                pe.wait_ge(s.mixedT_ready, index(p, 1))
                mm(s.scores[:, 1, 0:D], s.mixedT[:], w, True).then_inc(s.projected, 1)

            @for_live_pairs
            def gate_up(p):
                pe.wait_ge(F.inputT_ready, index(p, 1))
                if p.first >= 1:
                    pe.wait_ge(F.hidden_ready, index(p))
                for n, bank in ((0, F.gate), (1, F.up)):
                    for c in range(CHUNKS):
                        for half in range(2):
                            last = mm(bank[:, c * TOK:(c + 1) * TOK], w_in[:, n, c * 128:(c + 1) * 128], F.inputT[:, half], half == 0)
                last.then_inc(F.gate_up_ready, 1)

            @for_live_pairs
            def down(p):
                pe.wait_ge(F.hidden_low, index(p, 1))
                for c in range(CHUNKS):
                    for half in range(2):
                        last = mm(F.gate[:, 0:D], F.hidden16[:, half, c * TOK:(c + 1) * TOK], w_down[:, c * D:(c + 1) * D], c == 0 and half == 0)
                last.then_inc(F.down_ready, 1)

            def project_value_bias():
                pe.wait_ge(value_bias_ready, 1)
                mm(B.scores[:, 0, 0:D], value_bias_row[:], w_cross_out, True).then_inc(out_bias_projected, 1)

            def late_waits():
                pe.wait_ge(late_setup_done, 1)
                pe.wait_ge(out_bias_ready, 1)
                pe.wait_ge(cross_cleared, 1)

            def step(at):
                turn_max(A, at(2))
                turn_slots(A, at(1))
                scoresT_first(A, at(2))
                turn_cross(at(3))
                scoresT_rest(A, at(2))
                turn_self(at(0))
                project(B, w_cross_out, at(5))
                cross_qkv(at(3))
                scores(B, at(4))
                sum_weights(A, at(2))
                mix(A, at(2))
                down(at(8))
                turn_max(B, at(4))
                self_qkv(at(0))
                turn_slots(B, at(3))
                scoresT_first(B, at(4))
                turn_ffn(at(7))
                project(A, w_self_out, at(2))
                scoresT_rest(B, at(4))
                mask_scores(at(1))
                scores(A, at(1))
                gate_up(at(7))
                sum_weights(B, at(4))
                mix(B, at(4))

            run(pe, step, {2: project_value_bias, LAG_CROSS: late_waits})


def kernel(**inputs):
    import numpy as _np
    import concourse.bacc as _bacc
    from concourse import mybir as _mybir
    from concourse.bass_utils import run_bass_kernel_spmd as _run

    def flat(name):
        return _np.ascontiguousarray(_np.asarray(inputs[name]).reshape(-1, D))

    def turned(name):
        return _np.ascontiguousarray(_np.asarray(inputs[name]).T)

    def row(name):
        return _np.ascontiguousarray(_np.asarray(inputs[name]))

    arrays = {
        "x": flat("x"), "ctx": flat("ctx_1024"),
        "w_both": _np.concatenate([turned(n) for n in ("L0_attn_Wqkv", "L0_attn_Wo", "L0_xattn_W_q", "L0_xattn_W_k", "L0_xattn_W_v", "L0_xattn_W_o")], axis=1),
        "w_int": _np.stack([turned("L0_ffn_w_gate"), turned("L0_ffn_w_up"),
                            turned("L0_ffn_w_down").reshape(CHUNKS, 128, D).transpose(1, 0, 2).reshape(128, HIDDEN)], axis=1),
        "gates": _np.stack([row("L0_attn_log_xi"), row("L0_attn_pi_gate_logit"), row("L0_attn_e_gate_logit")]),
        "biases": _np.stack([row("L0_xattn_b_q"), row("L0_xattn_b_k"), row("L0_xattn_b_o")]),
        "value_bias": row("L0_xattn_b_v").reshape(D, 1),
        **constants(),
    }
    nc = _bacc.Bacc("TRN2", target_bir_lowering=False, num_devices=1)
    aps = {n: nc.dram_tensor(f"in_{n}", v.shape, _mybir.dt.from_np(v.dtype), kind="ExternalInput").ap() for n, v in arrays.items()}
    out = nc.dram_tensor("out_x", (BATCH * SEQ, D), F32, kind="ExternalOutput").ap()
    aps["out_flat"] = out
    build(nc, aps, out)
    r = _run(nc, [{f"in_{n}": v for n, v in arrays.items()}], core_ids=[0])
    return _np.asarray(r.results[0]["out_x"]).reshape(BATCH, SEQ, D)
```
